# Optimizing a Trainium2 kernel written in Bass

```python
import numpy as np
import jax
import jax.numpy as jnp

def _softmax(x, axis=-1):
    return jax.nn.softmax(x, axis=axis)

def _gelu(x):
    return jax.nn.gelu(x, approximate=True)

def _silu(x):
    return jax.nn.silu(x)

def _sigmoid(x):
    return jax.nn.sigmoid(x)

def _layernorm(x, axis=-1, eps=1e-05):
    m = jnp.mean(x, axis=axis, keepdims=True)
    v = jnp.var(x, axis=axis, keepdims=True)
    return (x - m) / jnp.sqrt(v + eps)

def _scatter_add(tgt, idx, src, axis=0):
    return tgt.at[idx].add(src)

def _segment_sum(src, seg, n):
    return jax.ops.segment_sum(src, seg, n)
kernel_name = 'mk_gnn_preln_d1_gnn_r64_ae5e61'

def setup_inputs(seed: int=0):
    np.random.seed(seed)
    _w = jnp.asarray

    def _rec_inputs():
        import jax
        import jax.numpy as jnp
        _gk = jax.random.key(seed)
        x = -0.0003713 + 1 * jax.random.normal(jax.random.fold_in(_gk, 1), (50000, 256), jnp.float32)
        _s = jax.random.randint(jax.random.fold_in(_gk, 2), (12500,), 0, 50000, jnp.int32)
        _d = jax.random.randint(jax.random.fold_in(_gk, 3), (12500,), 0, 50000, jnp.int32)
        _loop = jnp.arange(50000, dtype=jnp.int32)
        src = jnp.concatenate([_s, _d, _loop])
        dst = jnp.concatenate([_d, _s, _loop])
        _o = jnp.argsort(dst, stable=True)
        src = src[_o]
        dst = dst[_o]
        return (x, src, dst)
    x, src, dst = _rec_inputs()

    def _L0_gnn_setup():
        import jax, jax.numpy as jnp
        import numpy as np
        N, E = (50000, 12500)
        IN_DIM = 256
        OUT_DIM = 256
        H = 8
        D = OUT_DIM // H
        SCALE = D ** (-0.5)
        LN_EPS = 1e-05

        def _layernorm(x, g, b):
            mu = jnp.mean(x, axis=-1, keepdims=True)
            var = jnp.mean((x - mu) ** 2, axis=-1, keepdims=True)
            return (x - mu) * jax.lax.rsqrt(var + LN_EPS) * g + b
        key = jax.random.key(seed)
        ks = jax.random.split(key, 12)
        s = 1.0 / np.sqrt(IN_DIM)
        inp = {'x': jax.random.normal(ks[0], (N, IN_DIM), jnp.float32), 'edge_index': jax.random.randint(ks[1], (2, E), 0, N, jnp.int64), 'batch': jnp.zeros((N,), jnp.int64), 'Wq': jax.random.uniform(ks[2], (IN_DIM, OUT_DIM), jnp.float32, -s, s), 'Wk': jax.random.uniform(ks[3], (IN_DIM, OUT_DIM), jnp.float32, -s, s), 'Wv': jax.random.uniform(ks[4], (IN_DIM, OUT_DIM), jnp.float32, -s, s), 'Wo_w': jax.random.uniform(ks[5], (OUT_DIM, OUT_DIM), jnp.float32, -s, s), 'Wo_b': jnp.zeros((OUT_DIM,), jnp.float32), 'ln1_g': jnp.ones((OUT_DIM,), jnp.float32), 'ln1_b': jnp.zeros((OUT_DIM,), jnp.float32), 'ln2_g': jnp.ones((OUT_DIM,), jnp.float32), 'ln2_b': jnp.zeros((OUT_DIM,), jnp.float32), 'ffn_w1': jax.random.uniform(ks[6], (OUT_DIM, 2 * OUT_DIM), jnp.float32, -s, s), 'ffn_b1': jnp.zeros((2 * OUT_DIM,), jnp.float32), 'ffn_w2': jax.random.uniform(ks[7], (2 * OUT_DIM, OUT_DIM), jnp.float32, -s, s), 'ffn_b2': jnp.zeros((OUT_DIM,), jnp.float32)}
        return inp
    _L0_gnn_all = _L0_gnn_setup()
    _L0_gnn_in = {k: v for k, v in _L0_gnn_all.items() if k in ('Wq', 'Wk', 'Wv', 'Wo_w', 'Wo_b', 'ln1_g', 'ln1_b', 'ln2_g', 'ln2_b', 'ffn_w1', 'ffn_b1', 'ffn_w2', 'ffn_b2')}
    del _L0_gnn_all
    return {'x': x, 'src': src, 'dst': dst, 'L0_gnn_Wq': _L0_gnn_in['Wq'], 'L0_gnn_Wk': _L0_gnn_in['Wk'], 'L0_gnn_Wv': _L0_gnn_in['Wv'], 'L0_gnn_Wo_w': _L0_gnn_in['Wo_w'], 'L0_gnn_Wo_b': _L0_gnn_in['Wo_b'], 'L0_gnn_ln1_g': _L0_gnn_in['ln1_g'], 'L0_gnn_ln1_b': _L0_gnn_in['ln1_b'], 'L0_gnn_ln2_g': _L0_gnn_in['ln2_g'], 'L0_gnn_ln2_b': _L0_gnn_in['ln2_b'], 'L0_gnn_ffn_w1': _L0_gnn_in['ffn_w1'], 'L0_gnn_ffn_b1': _L0_gnn_in['ffn_b1'], 'L0_gnn_ffn_w2': _L0_gnn_in['ffn_w2'], 'L0_gnn_ffn_b2': _L0_gnn_in['ffn_b2']}

def reference(x, src, dst, L0_gnn_Wq, L0_gnn_Wk, L0_gnn_Wv, L0_gnn_Wo_w, L0_gnn_Wo_b, L0_gnn_ln1_g, L0_gnn_ln1_b, L0_gnn_ln2_g, L0_gnn_ln2_b, L0_gnn_ffn_w1, L0_gnn_ffn_b1, L0_gnn_ffn_w2, L0_gnn_ffn_b2):
    import jax
    import jax.numpy as jnp

    def _L0_gnn_ref(x, edge_index, batch, Wq, Wk, Wv, Wo_w, Wo_b, ln1_g, ln1_b, ln2_g, ln2_b, ffn_w1, ffn_b1, ffn_w2, ffn_b2):
        import jax, jax.numpy as jnp
        import numpy as np
        N, E = (50000, 12500)
        IN_DIM = 256
        OUT_DIM = 256
        H = 8
        D = OUT_DIM // H
        SCALE = D ** (-0.5)
        LN_EPS = 1e-05

        def _layernorm(x, g, b):
            mu = jnp.mean(x, axis=-1, keepdims=True)
            var = jnp.mean((x - mu) ** 2, axis=-1, keepdims=True)
            return (x - mu) * jax.lax.rsqrt(var + LN_EPS) * g + b
        n = x.shape[0]
        residual = x
        Q = (x @ Wq).reshape(n, H, D)
        K = (x @ Wk).reshape(n, H, D)
        V = (x @ Wv).reshape(n, H, D)
        src, dst = (edge_index[0], edge_index[1])
        scores = jnp.einsum('ehd,ehd->eh', Q[dst], K[src]) * SCALE
        attn_max = jnp.zeros((n, H), scores.dtype).at[dst].max(scores)
        w = jnp.exp(scores - attn_max[dst])
        attn_sum = jnp.zeros((n, H), w.dtype).at[dst].add(w)
        w = w / (attn_sum[dst] + 1e-08)
        msg = V[src] * w[:, :, None]
        out = jnp.zeros((n, H, D), msg.dtype).at[dst].add(msg)
        out = out.reshape(n, OUT_DIM) @ Wo_w + Wo_b
        out = _layernorm(residual + out, ln1_g, ln1_b)
        ffn = jax.nn.gelu(out @ ffn_w1 + ffn_b1, approximate=False) @ ffn_w2 + ffn_b2
        out = _layernorm(out + ffn, ln2_g, ln2_b)
        return out
    edge_index = jnp.stack([src, dst])
    batch0 = jnp.zeros((50000,), jnp.int32)
    h = jnp.maximum(_layernorm(x, axis=-1), 0.0)
    x = x + _L0_gnn_ref(h, edge_index, batch0, L0_gnn_Wq, L0_gnn_Wk, L0_gnn_Wv, L0_gnn_Wo_w, L0_gnn_Wo_b, L0_gnn_ln1_g, L0_gnn_ln1_b, L0_gnn_ln2_g, L0_gnn_ln2_b, L0_gnn_ffn_w1, L0_gnn_ffn_b1, L0_gnn_ffn_w2, L0_gnn_ffn_b2)
    return x

_drawn_inputs = setup_inputs


def setup_inputs(seed=0):
    import zlib

    import numpy as np

    out = dict(_drawn_inputs(seed))
    spreads = {'L0_gnn_Wo_b': (0.0, 0.1),
     'L0_gnn_ln1_g': (1.0, 0.2),
     'L0_gnn_ln1_b': (0.0, 0.1),
     'L0_gnn_ln2_g': (1.0, 0.2),
     'L0_gnn_ln2_b': (0.0, 0.1),
     'L0_gnn_ffn_b1': (0.0, 0.305),
     'L0_gnn_ffn_b2': (0.0, 0.1)}
    factors = {'L0_gnn_Wq': 8.0, 'L0_gnn_Wk': 8.0}
    for name, (base, spread) in spreads.items():
        noise = np.random.default_rng([zlib.crc32(name.encode()), seed]).standard_normal(out[name].shape)
        drawn = base * np.exp(spread * noise) if base else spread * noise
        out[name] = jnp.asarray(drawn.astype(out[name].dtype))
    for name, factor in factors.items():
        out[name] = (out[name] * factor).astype(out[name].dtype)
    return out
```

```python
from contextlib import ExitStack

import concourse.bass as bass
from concourse import mybir

P = 128
FEAT = 256
HEADS = 8
HEAD = FEAT // HEADS
HID = 512
KH = FEAT // P
HM = HID // P
GT = 4
SGT = 8
SGN = SGT * P
QS = FEAT + HEADS
SCALE = float(HEAD) ** -0.5
EPS = 1e-5
WIN = 3 * P
NO_SLOT = 70000.0
PAD_DST = 200000
PAD_SRC = 100000
HOLE = 0x007FFFFF
PACK = 23

fp32 = mybir.dt.float32
fp32r = mybir.dt.float32r
i32 = mybir.dt.int32
u32 = mybir.dt.uint32
ALU = mybir.AluOpType
ACT = mybir.ActivationFunctionType
AX = mybir.AxisListType.X


def program(nc, x, src, dst, Wq, Wk, Wv, Wo, Wo_b, g1, b1, g2, b2, W1, fb1, W2, fb2, out):
    N = x.shape[0]
    E = src.shape[0]
    SG = -(-N // SGN)
    T = SG * SGT
    T0 = T - SGT
    LAP = SG * SGN - N
    NB = -(-T // P)
    NT = NB * P
    W = E // P + 4
    assert T + SGT <= NT and N < 65535 and N >= SGN and T0 * P < 32768 * 4

    qs_d = nc.dram_tensor("qs_table", [N, QS], fp32).ap()
    kv_d = nc.dram_tensor("kv_table", [N, 2 * FEAT], fp32).ap()
    ep_src = nc.dram_tensor("edges_src", [(W + 1) * P], i32).ap()
    ep_dst = nc.dram_tensor("edges_dst", [(W + 1) * P], i32).ap()
    agg_d = nc.dram_tensor("general_agg", [N, FEAT], fp32).ap()

    outer = ExitStack()
    with outer:
        keep = lambda n, s, d=fp32: outer.enter_context(nc.sbuf_tensor(n, s, d))
        ident = keep("ident", [P, P])
        colf = keep("colf", [P, P])
        idx_src = keep("idx_src", [P, NT], u32)
        idx_dst = keep("idx_dst", [P, NT], u32)
        slot_dst = keep("slot_dst", [P, NT])
        tile_row = keep("tile_row", [P, NT])
        sself = keep("sself", [P, T, HEADS])
        rstd_all = keep("rstd_all", [P, T])
        nbias_all = keep("nbias_all", [P, T])
        flag = keep("flag", [1, 1], i32)
        wo = [keep(f"wo{k}", [P, KH, FEAT], fp32r) for k in range(2)]
        w1 = [keep(f"w1{k}", [P, KH, HID], fp32r) for k in range(2)]
        w2 = keep("w2", [P, HM, FEAT])
        vec = keep("vec", [P, 6, FEAT])
        WOB, G1, B1, G2, B2, FB2 = range(6)
        hb1 = keep("hb1", [P, HM])
        b1col = keep("b1col", [P, KH])

        with ExitStack() as early:
            wqkv = [early.enter_context(nc.sbuf_tensor(f"wqkv{k}", [P, KH, 3 * FEAT], fp32r)) for k in range(2)]
            prepare(nc, locals())
            project(nc, locals())
        general(nc, locals())
        finish(nc, locals())


def tensors(nc, stack):
    return (lambda n, s, d=fp32: stack.enter_context(nc.sbuf_tensor(n, s, d)),
            lambda n, s, d=fp32: stack.enter_context(nc.psum_tensor(n, s, d)),
            lambda n: stack.enter_context(nc.semaphore(n)))


def prepare(nc, env):
    (x, src, dst, ident, colf, idx_src, idx_dst, slot_dst, flag, vec, hb1, b1col, ep_src, ep_dst) = (
        env[k] for k in "x src dst ident colf idx_src idx_dst slot_dst flag vec hb1 b1col ep_src ep_dst".split())
    N, E, T, T0, LAP, NB, NT, W = (env[k] for k in "N E T T0 LAP NB NT W".split())
    PADS = (W + 1) * P - E
    SPLIT = next(d for d in range(16, 0, -1) if E % d == 0)
    weights = [(env["Wq"], env["wqkv"], 0, FEAT), (env["Wk"], env["wqkv"], FEAT, FEAT),
               (env["Wv"], env["wqkv"], 2 * FEAT, FEAT), (env["Wo"], env["wo"], 0, FEAT),
               (env["W1"], env["w1"], 0, HID)]
    with ExitStack() as stack:
        sb, ps, sem = tensors(nc, stack)
        raw = [sb(f"raw{i}", [P, w.shape[0] // P, w.shape[1]]) for i, (w, _, _, _) in enumerate(weights)]
        padd = sb("padd", [1, PADS], i32)
        pads = sb("pads", [1, PADS], i32)
        coli = sb("coli", [P, P], i32)
        rowi = sb("rowi", [P, NT], i32)
        bpi = sb("bpi", [P, NB], i32)
        posi = sb("posi", [P, WIN], i32)
        rowf = env["tile_row"]
        rowl = sb("rowl", [P, NT])
        bp = sb("bp", [P, 2, NB])
        bpl = sb("bpl", [P, NB])
        posf = sb("posf", [P, WIN])
        ones = sb("ones", [P, P])
        de = sb("de", [P, W], i32)
        dn = sb("dn", [P, W], i32)
        se = sb("se", [P, W], i32)
        ta = sb("ta", [P, W])
        tb = sb("tb", [P, W])
        sums = sb("sums", [P, 3])
        cmpm = sb("cmpm", [P, 2, NT])
        first = sb("first", [P, 1])
        coarse = sb("coarse", [P, 2 * NB])
        crow = sb("crow", [P, 2 * NB], u32)
        rowbuf = sb("rowbuf", [P, 2, W], i32)
        start = sb("start", [P, 2, NB])
        cnt = sb("cnt", [P, 2 * NB])
        st_i = sb("st_i", [P, NB], i32)
        c0 = sb("c0", [P, 3, NB], i32)
        c0f = sb("c0f", [P, NB])
        c0u = sb("c0u", [P, 3, NB], u32)
        off = sb("off", [P, NB])
        wsrc = sb("wsrc", [P, NB, WIN], i32)
        wdst = sb("wdst", [P, NB, WIN], i32)
        dl = sb("dl", [P, NB, WIN])
        va = sb("va", [P, NB, WIN])
        vb = sb("vb", [P, NB, WIN])
        mi = sb("mi", [P, NB, WIN], i32)
        vi = sb("vi", [P, NB, WIN], i32)
        vo = sb("vo", [P, NB, WIN], i32)
        hole = sb("hole", [P, NB, WIN], i32)
        tot = sb("tot", [1, 4])
        g1col = sb("g1col", [P, KH])
        bias_ready = sem("hidden_bias_ready")
        pc = ps("pc", [P, 512])
        pb = ps("pb", [P, 512])
        pt = [ps("pt0", [P, 512]), ps("pt1", [P, 512])]
        loaded = sem("weights_loaded")
        vecs = sem("vectors_loaded")
        consts = sem("constants_made")
        wiped = sem("windows_wiped")
        padded = sem("edges_padded")
        edges = sem("edges_loaded")
        own = sem("dve_own")
        cmp_ready = sem("compare_ready")
        coarse_ready = sem("coarse_ready")
        crow_ready = sem("coarse_row_ready")
        row_loaded = [sem("row_loaded0"), sem("row_loaded1")]
        row_used = sem("row_used")
        c0_ready = sem("window_row_ready")
        win_loaded = sem("window_loaded")
        sums_ready = sem("sums_ready")
        tot_ready = sem("totals_ready")
        slots_ready = sem("slots_ready")
        slots_turned = sem("slots_turned")
        block = stack.enter_context(nc.Block())

        @block.sync
        def _(sp):
            sp.dma_start(ep_dst[0:E].rearrange("(a b) -> a b", a=SPLIT), dst.rearrange("(a b) -> a b", a=SPLIT)).then_inc(padded, 16)
            sp.dma_start(ep_src[0:E].rearrange("(a b) -> a b", a=SPLIT), src.rearrange("(a b) -> a b", a=SPLIT)).then_inc(padded, 16)
            sp.wait_ge(consts, 1)
            sp.dma_start(ep_dst[E:(W + 1) * P].rearrange("(a b) -> a b", a=1), padd[:, :]).then_inc(padded, 16)
            sp.dma_start(ep_src[E:(W + 1) * P].rearrange("(a b) -> a b", a=1), pads[:, :]).then_inc(padded, 16)
            sp.wait_ge(padded, 64)
            sp.dma_start(de[:, :], ep_dst[0:W * P].rearrange("(p c) -> p c", p=P)).then_inc(edges, 16)
            sp.dma_start(dn[:, :], ep_dst[1:W * P + 1].rearrange("(p c) -> p c", p=P)).then_inc(edges, 16)
            sp.dma_start(se[:, :], ep_src[0:W * P].rearrange("(p c) -> p c", p=P)).then_inc(edges, 16)

        @block.scalar
        def _(act):
            for i, (w, _, _, _) in enumerate(weights):
                act.dma_start(raw[i][:, :, :], w.rearrange("(k p) n -> p k n", p=P)).then_inc(loaded, 16)
            act.dma_start(env["w2"][:, :, :], env["W2"].rearrange("(k p) n -> p k n", p=P)).then_inc(loaded, 16)
            for i, v in enumerate([env["Wo_b"], env["g1"], env["b1"], env["g2"], env["b2"], env["fb2"]]):
                act.dma_start(vec[:, i, :], v.partition_broadcast(P)).then_inc(vecs, 16)
            act.dma_start(hb1[:, :], env["fb1"].rearrange("(m p) -> p m", p=P), allow_slow_non_contiguous=True).then_inc(vecs, 16)
            act.dma_start(b1col[:, :], env["b1"].rearrange("(m p) -> p m", p=P), allow_slow_non_contiguous=True).then_inc(vecs, 16)
            act.dma_start(g1col[:, :], env["g1"].rearrange("(m p) -> p m", p=P), allow_slow_non_contiguous=True).then_inc(vecs, 16)
            act.wait_ge(vecs, 16 * 9)

        @block.gpsimd
        def _(pool):
            nc.gpsimd.memset(padd[:, :], PAD_DST)
            nc.gpsimd.memset(pads[:, :], PAD_SRC).then_inc(consts, 1)
            nc.gpsimd.memset(ident[:, :], 0.0)
            nc.gpsimd.memset(ones[:, :], 1.0)
            nc.gpsimd.iota(coli[:, :], [[1, P]], base=0, channel_multiplier=0)
            nc.gpsimd.iota(rowi[:, :], [[P, NT]], base=0, channel_multiplier=0)
            nc.gpsimd.iota(bpi[:, :], [[P * P, NB]], base=0, channel_multiplier=P)
            nc.gpsimd.iota(posi[:, :], [[1, WIN]], base=0, channel_multiplier=0).then_inc(consts, 1)
            pool.wait_ge(consts, 2)
            nc.gpsimd.affine_select(out=ident[:, :], in_=ident[:, :], compare_op=ALU.not_equal, fill=1.0,
                                    base=0, pattern=[[-1, P]], channel_multiplier=1).then_inc(consts, 1)
            nc.gpsimd.memset(wsrc[:, :, :], 0)
            nc.gpsimd.memset(wdst[:, :, :], 0).then_inc(wiped, 1)
            pool.wait_ge(crow_ready, 1)
            pool.wait_ge(padded, 64)
            for k in range(2 * NB):
                if k >= 2:
                    pool.wait_ge(row_used, k - 1)
                nc.gpsimd.indirect_dma_start(
                    out=rowbuf[:, k % 2, :], out_offset=None, in_=ep_dst[0:W * P].rearrange("(p c) -> p c", p=P),
                    in_offset=bass.IndirectOffsetOnAxis(ap=crow[:, k:k + 1], axis=0)).then_inc(row_loaded[k % 2], 16)
            pool.wait_ge(c0_ready, 1)
            pool.wait_ge(wiped, 1)
            for k in range(NB):
                for r in range(3):
                    for buf, tab in ((wsrc, ep_src), (wdst, ep_dst)):
                        nc.gpsimd.indirect_dma_start(
                            out=buf[:, k, r * P:(r + 1) * P], out_offset=None,
                            in_=tab.rearrange("(r c) -> r c", c=P),
                            in_offset=bass.IndirectOffsetOnAxis(ap=c0u[:, r, k:k + 1], axis=0),
                            bounds_check=W, oob_is_err=False).then_inc(win_loaded, 16)

        @block.tensor
        def _(pe):
            pe.wait_ge(cmp_ready, 1)
            pe.wait_ge(consts, 2)
            for h in range(2):
                for k in range(NB):
                    c = h * NB + k
                    mm = nc.tensor.matmul(pc[:, c:c + 1], cmpm[:, h, k * P:(k + 1) * P], ones[:, 0:1], start=True, stop=True)
            mm.then_inc(coarse_ready, 1)
            pe.wait_ge(loaded, 16 * (len(weights) + 1))
            pe.wait_ge(vecs, 16 * 9)
            for m in range(HM):
                for k in range(KH):
                    mm = nc.tensor.matmul(pb[:, m:m + 1], raw[4][:, k, m * P:(m + 1) * P], b1col[:, k:k + 1],
                                          start=k == 0, stop=k == KH - 1)
            mm.then_inc(bias_ready, 1)
            pe.wait_ge(sums_ready, 1)
            nc.tensor.matmul(pc[:, 64:67], ones[:, :], sums[:, :], start=True, stop=True).then_inc(tot_ready, 1)
            pe.wait_ge(slots_ready, 1)
            pe.wait_ge(consts, 3)
            for q, buf in enumerate((va, vb)):
                for k in range(NB):
                    tr = nc.tensor.transpose(pt[q][:, k * P:(k + 1) * P], buf[:, k, 0:P], ident[:, :])
            tr.then_inc(slots_turned, 1)

        @block.vector
        def _(v):
            done = [0]

            def seq(ins):
                done[0] += 1
                ins.then_inc(own, 1)
                v.wait_ge(own, done[0])

            v.wait_ge(consts, 2)
            seq(nc.vector.tensor_copy(colf[:, :], coli[:, :]))
            seq(nc.vector.tensor_copy(posf[:, :], posi[:, :]))
            seq(nc.vector.tensor_copy(rowf[:, :], rowi[:, :]))
            seq(nc.vector.tensor_copy(bp[:, 0, :], bpi[:, :]))
            seq(nc.vector.tensor_scalar(rowl[:, :], rowf[:, :], float(P * T0), float(-LAP), ALU.is_ge, ALU.mult))
            seq(nc.vector.tensor_tensor(rowf[:, :], rowf[:, :], rowl[:, :], ALU.add))
            seq(nc.vector.tensor_scalar(bpl[:, :], bp[:, 0, :], float(P * T0), float(-LAP), ALU.is_ge, ALU.mult))
            seq(nc.vector.tensor_tensor(bp[:, 0, :], bp[:, 0, :], bpl[:, :], ALU.add))
            seq(nc.vector.tensor_scalar(bp[:, 1, :], bp[:, 0, :], float(P), None, ALU.add))
            seq(nc.vector.memset(hole[:, :, :], HOLE))
            v.wait_ge(edges, 48)
            seq(nc.vector.tensor_copy(first[:, :], de[:, 0:1]))
            seq(nc.vector.tensor_scalar(cmpm[:, 0, :], rowf[:, :], first[:, 0:1], None, ALU.is_gt))
            seq(nc.vector.tensor_scalar(rowl[:, :], rowf[:, :], float(P), None, ALU.add))
            nc.vector.tensor_scalar(cmpm[:, 1, :], rowl[:, :], first[:, 0:1], None, ALU.is_gt).then_inc(cmp_ready, 1)
            seq(nc.vector.tensor_tensor(ta[:, :], dn[:, :], de[:, :], ALU.is_ge))
            seq(nc.vector.tensor_reduce(sums[:, 0:1], ta[:, :], AX, ALU.add))
            seq(nc.vector.tensor_tensor(ta[:, :], dn[:, :], de[:, :], ALU.not_equal))
            seq(nc.vector.tensor_tensor(tb[:, :], se[:, :], de[:, :], ALU.is_equal))
            seq(nc.vector.tensor_tensor(ta[:, :], ta[:, :], tb[:, :], ALU.mult))
            seq(nc.vector.tensor_reduce(sums[:, 1:2], ta[:, :], AX, ALU.add))
            v.wait_ge(coarse_ready, 1)
            seq(nc.vector.tensor_scalar(coarse[:, :], pc[:, 0:2 * NB], -1.0, 0.0, ALU.add, ALU.max))
            nc.vector.tensor_copy(crow[:, :], coarse[:, :]).then_inc(crow_ready, 1)
            for k in range(2 * NB):
                v.wait_ge(row_loaded[k % 2], 16 * (k // 2 + 1))
                seq(nc.vector.tensor_scalar(ta[:, :], rowbuf[:, k % 2, :], bp[:, k // NB, k % NB:k % NB + 1], None, ALU.is_lt))
                nc.vector.tensor_reduce(cnt[:, k:k + 1], ta[:, :], AX, ALU.add).then_inc(row_used, 1)
                v.wait_ge(row_used, k + 1)
            seq(nc.vector.scalar_tensor_tensor(start[:, :, :].rearrange("p a b -> p (a b)"), coarse[:, :], float(W),
                                               cnt[:, :], ALU.mult, ALU.add))
            seq(nc.vector.tensor_copy(st_i[:, :], start[:, 0, :]))
            seq(nc.vector.tensor_scalar(c0[:, 0, :], st_i[:, :], 7, None, ALU.logical_shift_right))
            seq(nc.vector.tensor_copy(c0f[:, :], c0[:, 0, :]))
            for r in range(3):
                ins = nc.vector.tensor_scalar(c0u[:, r, :], c0f[:, :], float(r), None, ALU.add)
            ins.then_inc(c0_ready, 1)
            seq(nc.vector.scalar_tensor_tensor(off[:, :], c0f[:, :], float(-P), start[:, 0, :], ALU.mult, ALU.add))
            seq(nc.vector.tensor_tensor(cnt[:, 0:NB], start[:, 1, :], start[:, 0, :], ALU.subtract))
            seq(nc.vector.tensor_scalar(cnt[:, 0:NB], cnt[:, 0:NB], float(2 * P), None, ALU.is_gt))
            nc.vector.tensor_reduce(sums[:, 2:3], cnt[:, 0:NB], AX, ALU.add).then_inc(sums_ready, 1)
            v.wait_ge(tot_ready, 1)
            seq(nc.vector.tensor_scalar(tot[:, 0:1], pc[0:1, 64:65], float(P * W), None, ALU.is_equal))
            seq(nc.vector.tensor_scalar(tot[:, 1:2], pc[0:1, 65:66], float(N), None, ALU.is_equal))
            seq(nc.vector.tensor_scalar(tot[:, 2:3], pc[0:1, 66:67], 0.0, None, ALU.is_equal))
            seq(nc.vector.tensor_tensor(tot[:, 0:1], tot[:, 0:1], tot[:, 1:2], ALU.mult))
            seq(nc.vector.tensor_tensor(tot[:, 0:1], tot[:, 0:1], tot[:, 2:3], ALU.mult))
            seq(nc.vector.tensor_scalar(flag[:, :], tot[:, 0:1], -1.0, 1.0, ALU.mult, ALU.add))
            v.wait_ge(vecs, 16 * 9)
            seq(nc.vector.tensor_tensor(vec[:, 5, :], vec[:, 5, :], vec[:, 2, :], ALU.add))
            v.wait_ge(loaded, 16 * (len(weights) + 1))
            v.wait_ge(bias_ready, 1)
            seq(nc.vector.tensor_tensor(hb1[:, :], hb1[:, :], pb[:, 0:HM], ALU.add))
            for k in range(KH):
                seq(nc.vector.tensor_scalar(raw[4][:, k, :], raw[4][:, k, :], g1col[:, k:k + 1], None, ALU.mult))
            for i, (_, parts, c, n) in enumerate(weights):
                seq(nc.vector.tensor_copy(parts[0][:, :, c:c + n], raw[i][:, :, :]))
                seq(nc.vector.tensor_tensor(parts[1][:, :, c:c + n], raw[i][:, :, :], parts[0][:, :, c:c + n].bitcast(fp32), ALU.subtract))
            v.wait_ge(win_loaded, 16 * 6 * NB)
            seq(nc.vector.tensor_tensor(dl[:, :, :], wdst[:, :, :], bp[:, 0, :].unsqueeze(2).broadcast_to([P, NB, WIN]), ALU.subtract))
            seq(nc.vector.memset(va[:, :, WIN - 1:WIN], 0.0))
            seq(nc.vector.tensor_tensor(va[:, :, 0:WIN - 1], wdst[:, :, 0:WIN - 1], wdst[:, :, 1:WIN], ALU.not_equal))
            seq(nc.vector.tensor_tensor(vb[:, :, :], wsrc[:, :, :], wdst[:, :, :], ALU.is_equal))
            seq(nc.vector.tensor_tensor(va[:, :, :], va[:, :, :], vb[:, :, :], ALU.mult))
            seq(nc.vector.tensor_scalar(vb[:, :, :], dl[:, :, :], 0.0, None, ALU.is_ge))
            seq(nc.vector.scalar_tensor_tensor(vb[:, :, :].rearrange("p k c -> p (k c)"), dl[:, :, :].rearrange("p k c -> p (k c)"), float(P),
                                               vb[:, :, :].rearrange("p k c -> p (k c)"), ALU.is_lt, ALU.mult))
            seq(nc.vector.tensor_scalar(va[:, :, :], va[:, :, :], -1.0, 1.0, ALU.mult, ALU.add))
            seq(nc.vector.tensor_tensor(va[:, :, :], va[:, :, :], vb[:, :, :], ALU.mult))
            seq(nc.vector.tensor_scalar(mi[:, :, :], va[:, :, :], -1.0, 1.0, ALU.mult, ALU.add))
            seq(nc.vector.tensor_tensor(vb[:, :, :], dl[:, :, :], off[:, :].unsqueeze(2).broadcast_to([P, NB, WIN]), ALU.add))
            seq(nc.vector.tensor_copy(vo[:, :, :], vb[:, :, :]))
            seq(nc.vector.tensor_scalar(vo[:, :, :], vo[:, :, :], PACK, None, ALU.logical_shift_left))
            seq(nc.vector.tensor_copy(vi[:, :, :], dl[:, :, :]))
            seq(nc.vector.tensor_tensor(vi[:, :, :], vi[:, :, :], vo[:, :, :], ALU.bitwise_or))
            seq(nc.vector.tensor_scalar(vo[:, :, :], wsrc[:, :, :], 7, None, ALU.logical_shift_left))
            seq(nc.vector.tensor_tensor(vi[:, :, :], vi[:, :, :], vo[:, :, :], ALU.bitwise_or))
            seq(nc.vector.copy_predicated(vi[:, :, :], mi[:, :, :], hole[:, :, :]))
            for b in range(8):
                d = 1 << b
                seq(nc.vector.tensor_scalar(mi[:, :, :], vi[:, :, :], PACK + b, 1, ALU.logical_shift_right, ALU.bitwise_and))
                seq(nc.vector.tensor_copy(vo[:, :, :], vi[:, :, :]))
                seq(nc.vector.copy_predicated(vi[:, :, :], mi[:, :, :], hole[:, :, :]))
                seq(nc.vector.copy_predicated(vi[:, :, 0:WIN - d], mi[:, :, d:WIN], vo[:, :, d:WIN]))
            seq(nc.vector.tensor_scalar(mi[:, :, 0:P], vi[:, :, 0:P], 7, 0xFFFF, ALU.logical_shift_right, ALU.bitwise_and))
            seq(nc.vector.tensor_copy(va[:, :, 0:P], mi[:, :, 0:P]))
            seq(nc.vector.tensor_scalar(vo[:, :, 0:P], vi[:, :, 0:P], 127, None, ALU.bitwise_and))
            seq(nc.vector.tensor_copy(dl[:, :, 0:P], vo[:, :, 0:P]))
            seq(nc.vector.tensor_scalar(vb[:, :, 0:P], va[:, :, 0:P], 65535.0, NO_SLOT, ALU.is_equal, ALU.mult))
            nc.vector.tensor_tensor(vb[:, :, 0:P], vb[:, :, 0:P], dl[:, :, 0:P], ALU.add).then_inc(slots_ready, 1)
            v.wait_ge(slots_turned, 1)
            nc.vector.tensor_copy(idx_src[:, :], pt[0][:, 0:NT])
            seq(nc.vector.tensor_copy(slot_dst[:, :], pt[1][:, 0:NT]))
            seq(nc.vector.tensor_tensor(idx_dst[:, :], slot_dst[:, :], rowf[:, :], ALU.add))


RSQRT_SEED = float(0x5F3759DF)
LN_STEPS = 18


def inverse_deviation(nc, v, own, base, stat, tmp, tmpi, rstd, nbias):
    mean_e, m2_e, mean_o, m2_o = (stat[:, :, k] for k in (1, 2, 4, 5))
    total, diff, var, root, corr = (tmp[:, k, :] for k in range(5))
    nc.vector.tensor_tensor(total, mean_e, mean_o, ALU.add).then_inc(own, 1)
    nc.vector.tensor_tensor(diff, mean_e, mean_o, ALU.subtract).then_inc(own, 1)
    nc.vector.tensor_tensor(var, m2_e, m2_o, ALU.add).then_inc(own, 1)
    v.wait_ge(own, base + 3)
    nc.vector.scalar_tensor_tensor(diff, diff, 0.25, diff, ALU.mult, ALU.mult).then_inc(own, 1)
    v.wait_ge(own, base + 4)
    nc.vector.scalar_tensor_tensor(var, var, 1.0 / FEAT, diff, ALU.mult, ALU.add).then_inc(own, 1)
    v.wait_ge(own, base + 5)
    nc.vector.tensor_scalar(var, var, EPS, None, ALU.add).then_inc(own, 1)
    v.wait_ge(own, base + 6)
    nc.vector.tensor_scalar(tmpi[:, :], var.bitcast(i32), 1, None, ALU.logical_shift_right).then_inc(own, 1)
    v.wait_ge(own, base + 7)
    nc.vector.tensor_scalar(root.bitcast(i32), tmpi[:, :], -1.0, RSQRT_SEED, ALU.mult, ALU.add).then_inc(own, 1)
    for k in range(3):
        v.wait_ge(own, base + 8 + 3 * k)
        nc.vector.scalar_tensor_tensor(corr, root, -0.5, root, ALU.mult, ALU.mult).then_inc(own, 1)
        v.wait_ge(own, base + 9 + 3 * k)
        nc.vector.tensor_tensor(corr, corr, var, ALU.mult).then_inc(own, 1)
        v.wait_ge(own, base + 10 + 3 * k)
        nc.vector.scalar_tensor_tensor(rstd if k == 2 else root, corr, 1.5, root, ALU.add, ALU.mult).then_inc(own, 1)
    v.wait_ge(own, base + 17)
    nc.vector.scalar_tensor_tensor(nbias, total, -0.5, rstd, ALU.mult, ALU.mult).then_inc(own, 1)


def project(nc, env):
    x, qs_d, kv_d, ident, sself, rstd_all, nbias_all, wqkv = (
        env[k] for k in "x qs_d kv_d ident sself rstd_all nbias_all wqkv".split())
    N, SG = env["N"], env["SG"]
    with ExitStack() as stack:
        sb, ps, sem = tensors(nc, stack)
        xg = [sb(f"xg{b}", [P, GT, FEAT]) for b in range(2)]
        hg = [sb(f"hg{b}", [P, GT, FEAT]) for b in range(2)]
        ht = [[sb(f"ht{b}{k}", [P, KH, GT * P], fp32r) for k in range(2)] for b in range(2)]
        qs = [sb(f"qs{b}", [P, GT, QS]) for b in range(2)]
        kv = [sb(f"kv{b}", [P, GT, 2 * FEAT]) for b in range(2)]
        prod = sb("prod", [P, GT, FEAT])
        stat = sb("stat", [P, GT, 6])
        tmp = sb("tmp", [P, 5, GT])
        tmpi = sb("tmpi", [P, GT], i32)
        rstd = [sb(f"rstd{b}", [P, GT]) for b in range(2)]
        nbias = [sb(f"nbias{b}", [P, GT]) for b in range(2)]
        tp = [ps(f"tp{k}", [P, 512]) for k in range(KH)]
        kvp = [ps(f"kvp{j}", [P, 512]) for j in range(GT)]
        qp = [ps(f"qp{j}", [P, 2, FEAT]) for j in range(2)]
        x_loaded = [sem("x_loaded0"), sem("x_loaded1")]
        qs_stored = [sem("qs_stored0"), sem("qs_stored1")]
        kv_stored = [sem("kv_stored0"), sem("kv_stored1")]
        own = sem("norm_steps")
        stats_own = sem("stats_done")
        norm_ready = sem("norm_ready")
        h_ready = sem("h_ready")
        turned = sem("h_turned")
        hi_ready = sem("ht_high_ready")
        lo_ready = sem("ht_low_ready")
        projected = sem("tile_projected")
        q_ready = sem("q_staged")
        kv_ready = sem("kv_staged")
        prod_ready = sem("score_products")
        score_ready = sem("own_scores_ready")
        block = stack.enter_context(nc.Block())
        own_steps = LN_STEPS

        def rows(i, b):
            first = (N - SGN) if isinstance(i, int) and i == SG - 1 else i * SGN
            return bass.ds(first + b * GT * P, GT * P)

        def every(eng, body):
            body(0)
            with eng.Fori(1, SG - 1) as i:
                body(i)
            body(SG - 1)

        @block.sync
        def _(sp):
            def load(i, b):
                if not (isinstance(i, int) and i == 0):
                    sp.wait_ge(h_ready, 2 * i + b - 1)
                sp.dma_start(xg[b][:, :, :], x[rows(i, b), :].rearrange("(j p) c -> p j c", p=P)).then_inc(x_loaded[b], 16)

            def store(i, b):
                sp.wait_ge(score_ready, 2 * i + b + 1)
                sp.dma_start(qs_d[rows(i, b), :].rearrange("(j p) c -> p j c", p=P), qs[b][:, :, :]).then_inc(qs_stored[b], 16)
                sp.wait_ge(kv_ready, GT * (2 * i + b + 1))
                sp.dma_start(kv_d[rows(i, b), :].rearrange("(j p) c -> p j c", p=P), kv[b][:, :, :]).then_inc(kv_stored[b], 16)

            load(0, 0)
            load(0, 1)
            load(1, 0)
            with sp.Fori(0, SG - 3) as i:
                load(i + 1, 1)
                store(i, 0)
                load(i + 2, 0)
                store(i, 1)
            load(SG - 2, 1)
            store(SG - 3, 0)
            load(SG - 1, 0)
            store(SG - 3, 1)
            load(SG - 1, 1)
            store(SG - 2, 0)
            store(SG - 2, 1)
            i = SG - 1
            for b in range(2):
                sp.wait_ge(qs_stored[b], 16 * i)
                sp.wait_ge(kv_stored[b], 16 * i)
            store(i, 0)
            store(i, 1)
            for b in range(2):
                sp.wait_ge(qs_stored[b], 16 * SG)
                sp.wait_ge(kv_stored[b], 16 * SG)

        @block.vector
        def _(v):
            def norm(i, b, t):
                g = 2 * i + b
                v.wait_ge(x_loaded[b], 16 * (i + 1))
                for j in range(GT):
                    st = nc.vector.bn_stats(stat[:, j, :], xg[b][:, j, :])
                st.then_inc(stats_own, 1)
                v.wait_ge(stats_own, g + 1)
                if not (isinstance(i, int) and i == 0):
                    v.wait_ge(h_ready, g - 1)
                inverse_deviation(nc, v, own, own_steps * g, stat, tmp, tmpi, rstd[b][:, :], nbias[b][:, :])
                v.wait_ge(own, own_steps * (g + 1))
                nc.vector.tensor_copy(rstd_all[:, bass.ds(t, GT)], rstd[b][:, :])
                nc.vector.tensor_copy(nbias_all[:, bass.ds(t, GT)], nbias[b][:, :]).then_inc(norm_ready, 1)

            def low(i, b):
                g = 2 * i + b
                for k in range(KH):
                    v.wait_ge(hi_ready, KH * g + k + 1)
                    nc.vector.tensor_tensor(ht[b][1][:, k, :], tp[k][:, :], ht[b][0][:, k, :].bitcast(fp32),
                                            ALU.subtract).then_inc(lo_ready, 1)

            def scores(i, b, t):
                g = 2 * i + b
                v.wait_ge(q_ready, 2 * (g + 1))
                if not (isinstance(i, int) and i == 0 and b == 0):
                    v.wait_ge(score_ready, g)
                nc.vector.tensor_tensor(prod[:, :, :], kv[b][:, :, 0:FEAT], qs[b][:, :, 0:FEAT], ALU.mult).then_inc(prod_ready, 1)
                v.wait_ge(prod_ready, g + 1)
                nc.vector.tensor_reduce(qs[b][:, :, FEAT:QS], prod[:, :, :].rearrange("p j (h d) -> p j h d", d=HEAD),
                                        AX, ALU.add).then_inc(score_ready, 1)
                v.wait_ge(score_ready, g + 1)
                nc.vector.tensor_copy(sself[:, bass.ds(t, GT), :], qs[b][:, :, FEAT:QS])

            def body(i):
                final = isinstance(i, int) and i == SG - 1
                for b in range(2):
                    if not (final and b == 1):
                        low(*((i, 1) if b == 0 else (i + 1, 0)))
                    if not final:
                        norm(i + 1, b, SGT * (i + 1) + GT * b)
                    scores(i, b, SGT * i + GT * b)

            norm(0, 0, 0)
            norm(0, 1, GT)
            low(0, 0)
            every(v, body)

        @block.scalar
        def _(act):
            def make_h(i, b):
                g = 2 * i + b
                act.wait_ge(norm_ready, g + 1)
                if not (isinstance(i, int) and i == 0):
                    act.wait_ge(turned, KH * (g - 1))
                for j in range(GT):
                    ins = nc.scalar.activation(hg[b][:, j, :], xg[b][:, j, :], ACT.Relu, bias=nbias[b][:, j:j + 1],
                                               scale=rstd[b][:, j:j + 1])
                ins.then_inc(h_ready, 1)

            def high(i, b):
                g = 2 * i + b
                if not (isinstance(i, int) and i == 0):
                    act.wait_ge(projected, GT * (g - 1))
                for k in range(KH):
                    act.wait_ge(turned, KH * g + k + 1)
                    nc.scalar.activation(ht[b][0][:, k, :], tp[k][:, :], ACT.Copy).then_inc(hi_ready, 1)

            def stage(i, b):
                g = 2 * i + b
                if not (isinstance(i, int) and i == 0):
                    act.wait_ge(qs_stored[b], 16 * i)
                    act.wait_ge(kv_stored[b], 16 * i)
                for j in range(GT):
                    act.wait_ge(projected, GT * g + j + 1)
                    nc.scalar.activation(kv[b][:, j, :], kvp[j][:, :], ACT.Copy).then_inc(kv_ready, 1)
                    if j % 2:
                        nc.scalar.activation(qs[b][:, j - 1:j + 1, 0:FEAT], qp[j // 2][:, :, :], ACT.Copy).then_inc(q_ready, 1)

            def body(i):
                final = isinstance(i, int) and i == SG - 1
                for b in range(2):
                    if not (final and b == 1):
                        high(*((i, 1) if b == 0 else (i + 1, 0)))
                    if not final:
                        make_h(i + 1, b)
                    stage(i, b)

            make_h(0, 0)
            make_h(0, 1)
            high(0, 0)
            every(act, body)

        @block.tensor
        def _(pe):
            def turn(i, b):
                g = 2 * i + b
                pe.wait_ge(h_ready, g + 1)
                for k in range(KH):
                    if not (isinstance(i, int) and i == 0 and b == 0):
                        pe.wait_ge(lo_ready, KH * (g - 1) + k + 1)
                    for j in range(GT):
                        tr = nc.tensor.transpose(tp[k][:, j * P:(j + 1) * P], hg[b][:, j, k * P:(k + 1) * P], ident[:, :])
                    tr.then_inc(turned, 1)

            def multiply(i, b):
                g = 2 * i + b
                pe.wait_ge(lo_ready, KH * (g + 1))
                for j in range(GT):
                    if not (isinstance(i, int) and i == 0 and b == 0):
                        pe.wait_ge(kv_ready, GT * (g - 1) + j + 1)
                        if j % 2 == 0:
                            pe.wait_ge(q_ready, 2 * (g - 1) + j // 2 + 1)
                    n = 0
                    for k in range(KH):
                        for a, w in ((0, 0), (0, 1), (1, 0)):
                            lhs = ht[b][a][:, k, j * P:(j + 1) * P]
                            nc.tensor.matmul(qp[j // 2][:, j % 2, :], lhs, wqkv[w][:, k, 0:FEAT], start=n == 0, stop=n == 5)
                            mm = nc.tensor.matmul(kvp[j][:, :], lhs, wqkv[w][:, k, FEAT:3 * FEAT], start=n == 0, stop=n == 5)
                            n += 1
                    mm.then_inc(projected, 1)

            def body(i):
                for b in range(2):
                    if isinstance(i, int) and i == 0 and b == 0:
                        turn(0, 0)
                    nxt = (i, 1) if b == 0 else (i + 1, 0)
                    if not (isinstance(i, int) and i == SG - 1 and b == 1):
                        turn(*nxt)
                    multiply(i, b)

            every(pe, body)


def general(nc, env):
    (ident, colf, tile_row, idx_src, idx_dst, slot_dst, sself, flag, qs_d, kv_d, ep_src, ep_dst, agg_d) = (
        env[k] for k in "ident colf tile_row idx_src idx_dst slot_dst sself flag qs_d kv_d ep_src ep_dst agg_d".split())
    N, E, T, T0, LAP = (env[k] for k in "N E T T0 LAP".split())
    C = -(-E // P)
    with ExitStack() as stack:
        sb, ps, sem = tensors(nc, stack)
        ids = sb("ids", [P, 2], i32)
        idu = sb("idu", [P, 2], u32)
        nought = sb("nought", [P, 2], i32)
        eq = sb("eq", [P, QS])
        ekv = sb("ekv", [P, 2 * FEAT])
        eqk = sb("eqk", [P, FEAT])
        base = sb("base", [P, 1])
        rel = sb("rel", [P, 1])
        score = sb("score", [P, HEADS])
        pos = sb("pos", [P, HEADS])
        ehot = sb("ehot", [P, P])
        spread = sb("spread", [P, HEADS, P])
        peak = sb("peak", [P, HEADS])
        gmax = sb("gmax", [P, HEADS])
        hot_t = sb("hot_t", [P, P])
        below = sb("below", [P, HEADS])
        wm = sb("wm", [P, QS])
        acc = sb("acc", [P, QS])
        inv = sb("inv", [P, HEADS])
        res = sb("res", [P, FEAT])
        spp = stack.enter_context(nc.psum_tensor("spp", [P, HEADS, P], fp32))
        otp = ps("otp", [P, 512])
        mep = ps("mep", [P, 512])
        sump = ps("sump", [P, 512])
        zeroed = sem("rows_zeroed")
        ids_free = sem("ids_free")
        ids_loaded = sem("ids_loaded")
        idu_ready = sem("indices_ready")
        rows_here = sem("rows_here")
        a_own = sem("max_steps")
        b_own = sem("sum_steps")
        spread_ready = sem("spread_ready")
        spread_turned = sem("spread_turned")
        hot_ready = sem("hot_ready")
        hot_turned = sem("hot_turned")
        hot_t_ready = sem("hot_t_ready")
        edge_max = sem("edge_max")
        below_ready = sem("below_ready")
        weight_ready = sem("weight_ready")
        wm_ready = sem("wm_ready")
        summed = sem("chunk_summed")
        tile_own = sem("tile_steps")
        res_ready = sem("tile_result")
        res_stored = sem("tile_stored")
        rewritten = sem("values_rewritten")
        block = stack.enter_context(nc.Block())
        A_STEPS, B_STEPS, TILE_STEPS = 8, 5, 4

        def walk(eng, chunk, before=None, after=None):
            for lo, hi, back in ((0, T0, 0), (T0, T, LAP)):
                with eng.Fori(lo, hi) as t:
                    if before:
                        before(t)
                    for second in (0, 1):
                        with eng.Fori(0, C) as c:
                            chunk(2 * C * t + C * second + c, t, c, second)
                    if after:
                        after(t, P * t - back)

        @block.sync
        def _(sp):
            need = sp.value_load(flag[0:1, 0:1], min_val=0, max_val=1)
            with sp.If(need > 0):
                def chunk(s, t, c, second):
                    sp.wait_ge(ids_free, s + 1)
                    sp.dma_start(ids[:, 0:1], ep_src[bass.ds(P * c, P)].rearrange("(p a) -> p a", a=1)).then_inc(ids_loaded, 16)
                    sp.dma_start(ids[:, 1:2], ep_dst[bass.ds(P * c, P)].rearrange("(p a) -> p a", a=1)).then_inc(ids_loaded, 16)

                def after(t, row):
                    sp.wait_ge(res_stored, 16 * (t + 1))
                    sp.wait_ge(res_ready, t + 1)
                    sp.dma_start(agg_d[bass.ds(row, P), :], res[:, :]).then_inc(res_stored, 16)

                sp.sem_inc(ids_free, 1)
                sp.sem_inc(res_stored, 16)
                walk(sp, chunk, after=after)
                sp.wait_ge(res_stored, 16 * (T + 1))
                sp.dma_start(kv_d[:, FEAT:2 * FEAT], agg_d).then_inc(rewritten, 16)
                sp.wait_ge(rewritten, 16)

        @block.gpsimd
        def _(pool):
            top_row = pool.to_reg(N - 1)
            need = pool.value_load(flag[0:1, 0:1], min_val=0, max_val=1)
            with pool.If(need > 0):
                nc.gpsimd.memset(nought[:, :], 0).then_inc(zeroed, 1)
                nc.gpsimd.memset(eq[:, :], 0.0)
                nc.gpsimd.memset(ekv[:, :], 0.0).then_inc(zeroed, 1)
                pool.wait_ge(zeroed, 2)

                def chunk(s, t, c, second):
                    pool.wait_ge(ids_loaded, 32 * (s + 1))
                    nc.gpsimd.tensor_tensor(idu[:, :], ids[:, :].bitcast(u32), nought[:, :].bitcast(u32), ALU.add).then_inc(idu_ready, 1)
                    pool.wait_ge(zeroed, 2)
                    pool.wait_ge(idu_ready, s + 1)
                    nc.gpsimd.indirect_dma_start(out=eq[:, :], out_offset=None, in_=qs_d,
                                                 in_offset=bass.IndirectOffsetOnAxis(ap=idu[:, 1:2], axis=0),
                                                 bounds_check=top_row, oob_is_err=False).then_inc(rows_here, 16)
                    nc.gpsimd.indirect_dma_start(out=ekv[:, :], out_offset=None, in_=kv_d,
                                                 in_offset=bass.IndirectOffsetOnAxis(ap=idu[:, 0:1], axis=0),
                                                 bounds_check=top_row, oob_is_err=False).then_inc(rows_here, 16)

                walk(pool, chunk)
                nc.gpsimd.memset(sself[:, :, :], 0.0)
                nc.gpsimd.memset(slot_dst[:, :], NO_SLOT)
                nc.gpsimd.memset(idx_src[:, :], int(NO_SLOT))
                nc.gpsimd.memset(idx_dst[:, :], int(NO_SLOT))

        @block.scalar
        def _(act):
            need = act.value_load(flag[0:1, 0:1], min_val=0, max_val=1)
            with act.If(need > 0):
                def chunk(s, t, c, second):
                    if second:
                        act.wait_ge(below_ready, C * t + c + 1)
                        nc.scalar.activation(wm[:, FEAT:QS], below[:, :], ACT.Exp, scale=SCALE).then_inc(weight_ready, 1)

                walk(act, chunk)

        @block.tensor
        def _(pe):
            need = pe.value_load(flag[0:1, 0:1], min_val=0, max_val=1)
            with pe.If(need > 0):
                def chunk(s, t, c, second):
                    n = C * t + c
                    if not second:
                        pe.wait_ge(spread_ready, n + 1)
                        for h in range(HEADS):
                            tr = nc.tensor.transpose(spp[:, h, :], spread[:, h, :], ident[:, :])
                        tr.then_inc(spread_turned, 1)
                    else:
                        pe.wait_ge(hot_ready, n + 1)
                        nc.tensor.transpose(otp[:, 0:P], ehot[:, :], ident[:, :]).then_inc(hot_turned, 1)
                        pe.wait_ge(hot_t_ready, n + 1)
                        nc.tensor.matmul(mep[:, 0:HEADS], hot_t[:, :], gmax[:, :], start=True, stop=True).then_inc(edge_max, 1)
                        pe.wait_ge(wm_ready, n + 1)
                        nc.tensor.matmul(sump[:, 0:QS], ehot[:, :], wm[:, :], start=True, stop=True).then_inc(summed, 1)

                walk(pe, chunk)

        @block.vector
        def _(v):
            need = v.value_load(flag[0:1, 0:1], min_val=0, max_val=1)
            with v.If(need > 0):
                def before(t):
                    v.wait_ge(tile_own, TILE_STEPS * t + 1)
                    nc.vector.tensor_copy(base[:, :], tile_row[:, bass.ds(t, 1)]).then_inc(tile_own, 1)

                def chunk(s, t, c, second):
                    n = C * t + c
                    own, k = (b_own, B_STEPS * n) if second else (a_own, A_STEPS * n)
                    v.wait_ge(tile_own, TILE_STEPS * t + 2)
                    v.wait_ge(rows_here, 32 * (s + 1))
                    nc.vector.tensor_tensor(rel[:, :], ids[:, 1:2], base[:, :], ALU.subtract).then_inc(own, 1)
                    nc.vector.tensor_tensor(eqk[:, :], eq[:, 0:FEAT], ekv[:, 0:FEAT], ALU.mult).then_inc(own, 1)
                    v.wait_ge(own, k + 2)
                    nc.vector.tensor_reduce(score[:, :], eqk[:, :].rearrange("p (h d) -> p h d", d=HEAD), AX, ALU.add).then_inc(own, 1)
                    if not second:
                        nc.vector.tensor_scalar(ehot[:, :], colf[:, :], rel[:, 0:1], None, ALU.is_equal).then_inc(own, 1)
                        v.wait_ge(own, k + 4)
                        nc.vector.tensor_scalar(pos[:, :], score[:, :], 0.0, None, ALU.max).then_inc(own, 1)
                        v.wait_ge(own, k + 5)
                        nc.vector.tensor_tensor(spread[:, :, :], ehot[:, :].unsqueeze(1).broadcast_to([P, HEADS, P]),
                                                pos[:, :].unsqueeze(2).broadcast_to([P, HEADS, P]), ALU.mult).then_inc(spread_ready, 1)
                        v.wait_ge(spread_turned, n + 1)
                        nc.vector.tensor_reduce(peak[:, 0:4], spp[:, 0:4, :], AX, ALU.max).then_inc(own, 1)
                        nc.vector.tensor_reduce(peak[:, 4:8], spp[:, 4:8, :], AX, ALU.max).then_inc(own, 1)
                        v.wait_ge(own, k + 7)
                        nc.vector.tensor_tensor(gmax[:, :], gmax[:, :], peak[:, :], ALU.max).then_inc(own, 1)
                        v.wait_ge(own, k + 8)
                        nc.vector.tensor_copy(rel[:, :], base[:, :]).then_inc(ids_free, 1)
                    else:
                        nc.vector.tensor_scalar(ehot[:, :], colf[:, :], rel[:, 0:1], None, ALU.is_equal).then_inc(hot_ready, 1)
                        v.wait_ge(hot_turned, n + 1)
                        nc.vector.tensor_copy(hot_t[:, :], otp[:, 0:P]).then_inc(hot_t_ready, 1)
                        v.wait_ge(edge_max, n + 1)
                        v.wait_ge(own, k + 3)
                        nc.vector.tensor_tensor(score[:, :], score[:, :], mep[:, 0:HEADS], ALU.subtract).then_inc(own, 1)
                        v.wait_ge(own, k + 4)
                        nc.vector.tensor_scalar(below[:, :], score[:, :], 0.0, None, ALU.min).then_inc(below_ready, 1)
                        v.wait_ge(weight_ready, n + 1)
                        nc.vector.tensor_tensor(wm[:, 0:FEAT].rearrange("p (h d) -> p h d", d=HEAD),
                                                ekv[:, FEAT:2 * FEAT].rearrange("p (h d) -> p h d", d=HEAD),
                                                wm[:, FEAT:QS].unsqueeze(2).broadcast_to([P, HEADS, HEAD]), ALU.mult).then_inc(wm_ready, 1)
                        v.wait_ge(summed, n + 1)
                        nc.vector.tensor_tensor(acc[:, :], acc[:, :], sump[:, 0:QS], ALU.add).then_inc(own, 1)
                        v.wait_ge(own, k + 5)
                        nc.vector.tensor_copy(rel[:, :], base[:, :]).then_inc(ids_free, 1)

                def after(t, row):
                    k = TILE_STEPS * t + 2
                    nc.vector.tensor_scalar(inv[:, :], acc[:, FEAT:QS], 1e-8, None, ALU.add).then_inc(tile_own, 1)
                    v.wait_ge(tile_own, k + 1)
                    nc.vector.reciprocal(inv[:, :], inv[:, :]).then_inc(tile_own, 1)
                    v.wait_ge(tile_own, k + 2)
                    v.wait_ge(res_stored, 16 * (t + 1))
                    nc.vector.tensor_tensor(res[:, :].rearrange("p (h d) -> p h d", d=HEAD),
                                            acc[:, 0:FEAT].rearrange("p (h d) -> p h d", d=HEAD),
                                            inv[:, :].unsqueeze(2).broadcast_to([P, HEADS, HEAD]), ALU.mult).then_inc(res_ready, 1)
                    v.wait_ge(res_ready, t + 1)
                    nc.vector.memset(gmax[:, :], 0.0)
                    nc.vector.memset(acc[:, :], 0.0).then_inc(tile_own, 1)

                nc.vector.memset(gmax[:, :], 0.0)
                nc.vector.memset(acc[:, :], 0.0).then_inc(tile_own, 1)
                walk(v, chunk, before, after)


def finish(nc, env):
    (x, out, qs_d, kv_d, ident, colf, idx_src, idx_dst, slot_dst, sself, rstd_all, nbias_all, wo, w1, w2, vec, hb1) = (
        env[k] for k in ("x out qs_d kv_d ident colf idx_src idx_dst slot_dst sself rstd_all nbias_all "
                         "wo w1 w2 vec hb1").split())
    N, SG = env["N"], env["SG"]
    WOB, G1, B1, G2, B2, FB2 = range(6)
    SH = SGT * HEADS
    with ExitStack() as stack:
        sb, ps, sem = tensors(nc, stack)
        isrc = sb("isrc", [P, SGT], u32)
        idst = sb("idst", [P, SGT], u32)
        qg = sb("qg", [P, SGT, QS])
        kvg = sb("kvg", [P, SGT, 2 * FEAT])
        qk = sb("qk", [P, SGT, FEAT])
        tin = sb("tin", [P, 4, SGT, HEADS])
        own_t = sb("own_t", [SH, P])
        dst_t = sb("dst_t", [SH, P])
        same = sb("same", [SH, P + 1])
        last = sb("last", [SH, P])
        best = sb("best", [SH, P])
        run = sb("run", [SH, P])
        top = sb("top", [SH, P])
        less = sb("less", [SH, 2, P])
        ew = sb("ew", [SH, 2, P])
        den = sb("den", [SH, P])
        tback = sb("tback", [P, 3, P])
        pslot = sb("pslot", [P, SGT, HEADS])
        sel = sb("sel", [P, SGT, 2, HEADS])
        hot = sb("hot", [P, SGT, P])
        msg = sb("msg", [P, SGT, FEAT])
        alone = sb("alone", [P, 3, SGT, HEADS])
        pself = sb("pself", [P, SGT, HEADS])
        xg = [sb(f"x2g{b}", [P, GT, FEAT]) for b in range(2)]
        vrow = [sb(f"vrow{b}", [P, GT, FEAT]) for b in range(2)]
        xb = [sb(f"xb{b}", [P, GT, FEAT]) for b in range(2)]
        nrm = [sb(f"nrm{b}", [P, 2, GT]) for b in range(2)]
        hres = sb("hres", [P, GT, FEAT])
        agg = sb("agg", [P, GT, FEAT])
        at = [sb(f"at{k}", [P, KH, GT * P], fp32r) for k in range(2)]
        mid = sb("mid", [P, GT, FEAT])
        ot = [sb(f"ot{k}", [P, KH, GT * P], fp32r) for k in range(2)]
        res2 = [sb(f"res2{b}", [P, GT, FEAT]) for b in range(2)]
        hid = sb("hid", [P, HM, GT * P])
        fin = [sb(f"fin{b}", [P, GT, FEAT]) for b in range(2)]
        stat = [sb(f"stat_of{k}", [P, GT, 6]) for k in range(2)]
        tmp = [sb(f"tmp_of{k}", [P, 5, GT]) for k in range(2)]
        tmpi = [sb(f"tmpi_of{k}", [P, GT], i32) for k in range(2)]
        rstd = [sb(f"rstd_of{k}", [P, GT]) for k in range(2)]
        nbias = [sb(f"nbias_of{k}", [P, GT]) for k in range(2)]
        tp = [ps(f"tq{k}", [P, 512]) for k in range(KH)]
        segp = [ps(f"segp{k}", [P, 2, FEAT]) for k in range(2)]
        yp = [ps(f"yp{k}", [P, 2, FEAT]) for k in range(2)]
        hp = ps("hp", [P, 512])
        ap = ps("ap", [P, 512])
        chunk_bank = [hp, tp[0], tp[1], hp]
        x_loaded = [sem("x2_loaded0"), sem("x2_loaded1")]
        v_loaded = [sem("v_loaded0"), sem("v_loaded1")]
        stored = [sem("out_stored0"), sem("out_stored1")]
        gathered = sem("slots_gathered")
        cleared = sem("gather_cleared")
        att_own = sem("attention_steps")
        a_own = sem("agg_steps")
        n1_own = sem("norm1_steps")
        n2_own = sem("norm2_steps")
        tin_ready = sem("scores_ready")
        tin_turned = sem("scores_turned")
        less_ready = sem("differences_ready")
        exp_ready = sem("exponentials_ready")
        tback_ready = sem("weights_ready")
        tback_turned = sem("weights_turned")
        msg_ready = sem("messages_ready")
        sel_turned = sem("loops_selected")
        pself_ready = sem("loop_weights_ready")
        nrm_ready = sem("norm_staged")
        h_ready = sem("h_again")
        hres_ready = sem("residual_ready")
        xb_ready = sem("x_plus_b2")
        vself_ready = sem("own_values_weighted")
        seg_done = sem("segments_summed")
        agg_ready = sem("agg_ready")
        agg_turned = sem("agg_turned")
        at_hi = sem("at_high")
        at_lo = sem("at_low")
        wo_done = sem("projected_out")
        mid_sum = sem("residual_summed")
        z1_ready = sem("normed1")
        mid_scaled = sem("mid_scaled")
        mid_turned = sem("mid_turned")
        ot_hi = sem("ot_high")
        ot_lo = sem("ot_low")
        res2_ready = sem("residual2_ready")
        chunk_done = sem("hidden_chunk")
        gelu_done = sem("gelu_done")
        ffn_done = sem("ffn_done")
        fin_sum = sem("residual2_summed")
        z2_ready = sem("normed2")
        fin_ready = sem("out_ready")
        block = stack.enter_context(nc.Block())
        ATT = 21

        def is_first(i, b=0):
            return isinstance(i, int) and i == 0 and b == 0

        def is_last(i):
            return isinstance(i, int) and i == SG - 1

        def before(i, b):
            return (i, 0, 2 * i) if b else (i - 1, 1, 2 * i - 1)

        def every(eng, body):
            body(0)
            with eng.Fori(1, SG - 1) as i:
                body(i)
            body(SG - 1)

        def rows(i, b):
            first = (N - SGN) if is_last(i) else i * SGN
            return bass.ds(first + b * GT * P, GT * P)

        @block.sync
        def _(sp):
            def load(i, b):
                g = 2 * i + b
                if not (isinstance(i, int) and i == 0):
                    sp.wait_ge(h_ready, g - 1)
                    sp.wait_ge(xb_ready, g - 1)
                sp.dma_start(xg[b][:, :, :], x[rows(i, b), :].rearrange("(j p) c -> p j c", p=P)).then_inc(x_loaded[b], 16)
                if not (isinstance(i, int) and i == 0):
                    sp.wait_ge(agg_ready, 2 * (g - 1))
                sp.dma_start(vrow[b][:, :, :], kv_d[rows(i, b), FEAT:2 * FEAT].rearrange("(j p) c -> p j c", p=P)).then_inc(v_loaded[b], 16)

            def store(i, b):
                sp.wait_ge(fin_ready, 2 * i + b + 1)
                sp.dma_start(out[rows(i, b), :].rearrange("(j p) c -> p j c", p=P), fin[b][:, :, :]).then_inc(stored[b], 16)

            for b in range(2):
                sp.sem_inc(stored[b], 16)
            load(0, 0)
            load(0, 1)
            with sp.Fori(0, SG - 2) as i:
                load(i + 1, 0)
                store(i, 0)
                load(i + 1, 1)
                store(i, 1)
            load(SG - 1, 0)
            store(SG - 2, 0)
            load(SG - 1, 1)
            store(SG - 2, 1)
            for b in range(2):
                sp.wait_ge(stored[b], 16 * SG)
            store(SG - 1, 0)
            store(SG - 1, 1)
            for b in range(2):
                sp.wait_ge(stored[b], 16 * (SG + 1))

        @block.gpsimd
        def _(pool):
            top_row = pool.to_reg(N - 1)

            def gather(i, half):
                for t in range(GT * half, GT * half + GT):
                    nc.gpsimd.indirect_dma_start(
                        out=qg[:, t, :], out_offset=None, in_=qs_d,
                        in_offset=bass.IndirectOffsetOnAxis(ap=idst[:, t:t + 1], axis=0),
                        bounds_check=top_row, oob_is_err=False).then_inc(gathered, 16)
                    nc.gpsimd.indirect_dma_start(
                        out=kvg[:, t, :], out_offset=None, in_=kv_d,
                        in_offset=bass.IndirectOffsetOnAxis(ap=isrc[:, t:t + 1], axis=0),
                        bounds_check=top_row, oob_is_err=False).then_inc(gathered, 16)

            def weigh_own(i, b):
                pool.wait_ge(v_loaded[b], 16 * (i + 1))
                pool.wait_ge(pself_ready, i + 1)
                vh = vrow[b][:, :, :].rearrange("p j (h d) -> p (j h) d", d=HEAD)
                ph = pself[:, GT * b:GT * b + GT, :].rearrange("p j h -> p (j h)").unsqueeze(2).broadcast_to([P, GT * HEADS, HEAD])
                nc.gpsimd.tensor_tensor(vh, vh, ph, ALU.mult).then_inc(vself_ready, 1)

            def first_residual(i, b):
                pool.wait_ge(h_ready, 2 * i + b + 1)
                nc.gpsimd.tensor_tensor(hres[:, :, :], hres[:, :, :], vec[:, WOB, :].unsqueeze(1).broadcast_to([P, GT, FEAT]),
                                        ALU.add).then_inc(hres_ready, 1)

            def last_residual(i, b):
                pool.wait_ge(x_loaded[b], 16 * (i + 1))
                if not (isinstance(i, int) and i == 0):
                    pool.wait_ge(fin_ready, 2 * i + b - 1)
                nc.gpsimd.tensor_tensor(xb[b][:, :, :], xg[b][:, :, :], vec[:, B2, :].unsqueeze(1).broadcast_to([P, GT, FEAT]),
                                        ALU.add).then_inc(xb_ready, 1)

            def second_residual(i, b):
                pool.wait_ge(mid_scaled, 2 * i + b + 1)
                nc.gpsimd.tensor_tensor(res2[b][:, :, :], res2[b][:, :, :], vec[:, FB2, :].unsqueeze(1).broadcast_to([P, GT, FEAT]),
                                        ALU.add).then_inc(res2_ready, 1)

            nc.gpsimd.memset(qg[:, :, :], 0.0)
            nc.gpsimd.memset(kvg[:, :, :], 0.0).then_inc(cleared, 1)
            pool.wait_ge(cleared, 2)
            gather(0, 0)
            gather(0, 1)
            pool.wait_ge(msg_ready, 1)
            weigh_own(0, 0)
            gather(1, 0)

            def body(i):
                first_residual(i, 0)
                if not is_last(i):
                    gather(i + 1, 1)
                last_residual(i, 0)
                second_residual(i, 0)
                weigh_own(i, 1)
                first_residual(i, 1)
                last_residual(i, 1)
                second_residual(i, 1)
                if not is_last(i):
                    pool.wait_ge(msg_ready, i + 2)
                    weigh_own(i + 1, 0)

            body(0)
            gather(2, 0)
            with pool.Fori(1, SG - 2) as i:
                body(i)
                gather(i + 2, 0)
            body(SG - 2)
            body(SG - 1)

        @block.scalar
        def _(act):
            def h_again(i, b):
                g = 2 * i + b
                act.wait_ge(nrm_ready, g + 1)
                act.wait_ge(x_loaded[b], 16 * (i + 1))
                if not is_first(i, b):
                    act.wait_ge(mid_sum, 2 * g)
                for j in range(GT):
                    ins = nc.scalar.activation(hres[:, j, :], xg[b][:, j, :], ACT.Relu, bias=nrm[b][:, 1, j:j + 1],
                                               scale=nrm[b][:, 0, j:j + 1])
                ins.then_inc(h_ready, 1)

            def gelus(gp, first):
                for m in range(HM):
                    act.wait_ge(chunk_done, HM * gp + m + 1)
                    if not first and m == 0:
                        act.wait_ge(ffn_done, 2 * gp)
                    nc.scalar.activation(hid[:, m, :], chunk_bank[m][:, :], ACT.Gelu, bias=hb1[:, m:m + 1]).then_inc(gelu_done, 1)

            def agg_high(i, b):
                g = 2 * i + b
                for k in range(KH):
                    act.wait_ge(agg_turned, KH * g + k + 1)
                    if not is_first(i, b) and k == 0:
                        act.wait_ge(wo_done, 2 * g)
                    nc.scalar.activation(at[0][:, k, :], tp[k][:, :], ACT.Copy).then_inc(at_hi, 1)

            def exps(i):
                act.wait_ge(less_ready, i + 1)
                nc.scalar.activation(ew[:, :, :], less[:, :, :], ACT.Exp, scale=SCALE)
                nc.scalar.activation(alone[:, 1, :, :], alone[:, 0, :, :], ACT.Exp, scale=SCALE).then_inc(exp_ready, 1)

            def norm1(i, b):
                act.wait_ge(n1_own, (LN_STEPS + 1) * (2 * i + b + 1))
                for j in range(GT):
                    ins = nc.scalar.activation(mid[:, j, :], mid[:, j, :], ACT.Identity, bias=nbias[0][:, j:j + 1], scale=rstd[0][:, j:j + 1])
                ins.then_inc(z1_ready, 1)

            def mid_high(i, b):
                g = 2 * i + b
                for k in range(KH):
                    act.wait_ge(mid_turned, KH * g + k + 1)
                    if not is_first(i, b) and k == 0:
                        act.wait_ge(chunk_done, HM * g)
                    nc.scalar.activation(ot[0][:, k, :], tp[k][:, :], ACT.Copy).then_inc(ot_hi, 1)

            def norm2(gp, bp):
                act.wait_ge(n2_own, (LN_STEPS + 2) * gp + LN_STEPS + 1)
                for j in range(GT):
                    ins = nc.scalar.activation(fin[bp][:, j, :], fin[bp][:, j, :], ACT.Identity, bias=nbias[1][:, j:j + 1], scale=rstd[1][:, j:j + 1])
                ins.then_inc(z2_ready, 1)

            exps(0)
            h_again(0, 0)

            def body(i):
                for b in range(2):
                    _, bp, gp = before(i, b)
                    if not is_first(i, b):
                        gelus(gp, is_first(i))
                    agg_high(i, b)
                    if b == 1 and not is_last(i):
                        exps(i + 1)
                    norm1(i, b)
                    mid_high(i, b)
                    if not is_first(i, b):
                        norm2(gp, bp)
                    if b == 0:
                        h_again(i, 1)
                    elif not is_last(i):
                        h_again(i + 1, 0)

            every(act, body)
            gelus(2 * SG - 1, False)
            norm2(2 * SG - 1, 1)

        @block.vector
        def _(v):
            def stage_norm(i, b):
                g = 2 * i + b
                if not (isinstance(i, int) and i == 0):
                    v.wait_ge(h_ready, g - 1)
                nc.vector.tensor_copy(nrm[b][:, 0, :], rstd_all[:, bass.ds(SGT * i + GT * b, GT)])
                nc.vector.tensor_copy(nrm[b][:, 1, :], nbias_all[:, bass.ds(SGT * i + GT * b, GT)]).then_inc(nrm_ready, 1)

            def att_scores(i):
                v.wait_ge(gathered, 16 * 2 * SGT * (i + 1))
                if not is_first(i):
                    v.wait_ge(tin_turned, i)
                nc.vector.tensor_copy(tin[:, 1, :, :], qg[:, :, FEAT:QS])
                nc.vector.tensor_copy(tin[:, 2, :, :], slot_dst[:, bass.ds(SGT * i, SGT)].unsqueeze(2).broadcast_to([P, SGT, HEADS]))
                nc.vector.tensor_tensor(qk[:, :, :], qg[:, :, 0:FEAT], kvg[:, :, 0:FEAT], ALU.mult).then_inc(att_own, 1)
                v.wait_ge(att_own, ATT * i + 1)
                nc.vector.tensor_reduce(tin[:, 0, :, :], qk[:, :, :].rearrange("p t (h d) -> p t h d", d=HEAD), AX,
                                        ALU.add).then_inc(tin_ready, 1)

            def att_max(i):
                c = ATT * i
                v.wait_ge(tin_turned, i + 1)
                nc.vector.tensor_copy(own_t[:, :], ap[0:SH, P:2 * P]).then_inc(att_own, 1)
                nc.vector.tensor_copy(dst_t[:, :], ap[0:SH, 2 * P:3 * P]).then_inc(att_own, 1)
                v.wait_ge(att_own, c + 3)
                nc.vector.tensor_tensor(same[:, 1:P], dst_t[:, 1:P], dst_t[:, 0:P - 1], ALU.is_equal).then_inc(att_own, 1)
                nc.vector.scalar_tensor_tensor(best[:, :], ap[0:SH, 0:P], 0.0, own_t[:, :], ALU.max, ALU.max).then_inc(att_own, 1)
                nc.vector.tensor_scalar(alone[:, 0, :, :], sself[:, bass.ds(SGT * i, SGT), :], 0.0, None, ALU.min).then_inc(att_own, 1)
                v.wait_ge(att_own, c + 6)
                nc.vector.tensor_tensor_scan(run[:, :], same[:, 0:P], best[:, :], 0.0, ALU.mult, ALU.max).then_inc(att_own, 1)
                nc.vector.tensor_scalar(last[:, :], same[:, 1:P + 1], -1.0, 1.0, ALU.mult, ALU.add).then_inc(att_own, 1)
                v.wait_ge(att_own, c + 8)
                nc.vector.tensor_tensor_scan(top[:, ::-1], same[:, P:0:-1], run[:, ::-1], 0.0, ALU.mult, ALU.max).then_inc(att_own, 1)
                v.wait_ge(att_own, c + 9)
                nc.vector.tensor_tensor(less[:, 0, :], ap[0:SH, 0:P], top[:, :], ALU.subtract)
                nc.vector.tensor_tensor(less[:, 1, :], own_t[:, :], top[:, :], ALU.subtract).then_inc(less_ready, 1)

            def att_weights(i):
                c = ATT * i + 9
                v.wait_ge(exp_ready, i + 1)
                nc.vector.tensor_tensor_scan(run[:, :], same[:, 0:P], ew[:, 0, :], 0.0, ALU.mult, ALU.add).then_inc(att_own, 1)
                nc.vector.tensor_scalar(alone[:, 2, :, :], alone[:, 1, :, :], 1e-8, None, ALU.add).then_inc(att_own, 1)
                v.wait_ge(att_own, c + 2)
                nc.vector.tensor_tensor_scan(top[:, ::-1], same[:, P:0:-1], run[:, ::-1], 0.0, ALU.mult, ALU.max).then_inc(att_own, 1)
                nc.vector.reciprocal(alone[:, 2, :, :], alone[:, 2, :, :]).then_inc(att_own, 1)
                v.wait_ge(att_own, c + 4)
                nc.vector.scalar_tensor_tensor(den[:, :], top[:, :], 1e-8, ew[:, 1, :], ALU.add, ALU.add).then_inc(att_own, 1)
                nc.vector.tensor_tensor(alone[:, 0, :, :], alone[:, 1, :, :], alone[:, 2, :, :], ALU.mult).then_inc(att_own, 1)
                v.wait_ge(att_own, c + 6)
                nc.vector.reciprocal(den[:, :], den[:, :]).then_inc(att_own, 1)
                v.wait_ge(att_own, c + 7)
                if not is_first(i):
                    v.wait_ge(tback_turned, i)
                nc.vector.tensor_tensor(tback[0:SH, 0, :], ew[:, 0, :], den[:, :], ALU.mult).then_inc(att_own, 1)
                nc.vector.tensor_tensor(tback[0:SH, 1, :], ew[:, 1, :], den[:, :], ALU.mult).then_inc(att_own, 1)
                v.wait_ge(att_own, c + 9)
                nc.vector.tensor_tensor(tback[0:SH, 1, :], tback[0:SH, 1, :], last[:, :], ALU.mult)
                nc.vector.tensor_copy(tback[0:SH, 2, :], last[:, :]).then_inc(tback_ready, 1)

            def att_messages(i):
                c = ATT * i + 18
                v.wait_ge(tback_turned, i + 1)
                nc.vector.tensor_copy(pslot[:, :, :], ap[:, 0:SH].rearrange("p (t h) -> p t h", h=HEADS)).then_inc(att_own, 1)
                if not is_first(i):
                    v.wait_ge(sel_turned, i)
                    v.wait_ge(seg_done, 4 * i)
                nc.vector.tensor_copy(sel[:, :, 0, :], ap[:, SH:2 * SH].rearrange("p (t h) -> p t h", h=HEADS))
                nc.vector.tensor_copy(sel[:, :, 1, :], ap[:, 2 * SH:3 * SH].rearrange("p (t h) -> p t h", h=HEADS))
                for t in range(SGT):
                    nc.vector.tensor_scalar(hot[:, t, :], colf[:, :], tin[:, 2, t, 0:1], None, ALU.is_equal)
                nc.vector.tensor_copy(isrc[:, :], idx_src[:, bass.ds(SGT * i + SGT, SGT)])
                nc.vector.tensor_copy(idst[:, :], idx_dst[:, bass.ds(SGT * i + SGT, SGT)])
                v.wait_ge(att_own, c + 1)
                nc.vector.tensor_tensor(
                    msg[:, :, :].rearrange("p t (h d) -> p t h d", d=HEAD),
                    kvg[:, :, FEAT:2 * FEAT].rearrange("p t (h d) -> p t h d", d=HEAD),
                    pslot[:, :, :].unsqueeze(3).broadcast_to([P, SGT, HEADS, HEAD]), ALU.mult).then_inc(msg_ready, 1)

            def att_own_weights(i):
                c = ATT * i + 19
                got = ap[:, 256:256 + 2 * SH].rearrange("p (t s h) -> p t s h", s=2, h=HEADS)
                v.wait_ge(sel_turned, i + 1)
                nc.vector.tensor_scalar(alone[:, 1, :, :], got[:, :, 1, :], -1.0, 1.0, ALU.mult, ALU.add).then_inc(att_own, 1)
                v.wait_ge(att_own, c + 1)
                nc.vector.tensor_tensor(alone[:, 2, :, :], alone[:, 1, :, :], alone[:, 0, :, :], ALU.mult).then_inc(att_own, 1)
                v.wait_ge(att_own, c + 2)
                if not is_first(i):
                    v.wait_ge(vself_ready, 2 * i)
                nc.vector.tensor_tensor(pself[:, :, :], alone[:, 2, :, :], got[:, :, 0, :], ALU.add).then_inc(pself_ready, 1)

            def sum_agg(i, b):
                g = 2 * i + b
                v.wait_ge(vself_ready, g + 1)
                if not is_first(i, b):
                    v.wait_ge(agg_turned, KH * g)
                for k in range(2):
                    v.wait_ge(seg_done, 2 * g + k + 1)
                    nc.vector.tensor_tensor(agg[:, 2 * k:2 * k + 2, :], segp[k][:, :, :], vrow[b][:, 2 * k:2 * k + 2, :], ALU.add).then_inc(agg_ready, 1)

            def agg_low(i, b):
                g = 2 * i + b
                for k in range(KH):
                    v.wait_ge(at_hi, KH * g + k + 1)
                    nc.vector.tensor_tensor(at[1][:, k, :], tp[k][:, :], at[0][:, k, :].bitcast(fp32), ALU.subtract).then_inc(at_lo, 1)

            def sum_mid(i, b):
                g = 2 * i + b
                v.wait_ge(hres_ready, g + 1)
                if not is_first(i, b):
                    v.wait_ge(mid_turned, KH * g)
                    v.wait_ge(mid_scaled, g)
                for k in range(2):
                    v.wait_ge(wo_done, 2 * g + k + 1)
                    nc.vector.tensor_tensor(mid[:, 2 * k:2 * k + 2, :], segp[k][:, :, :], hres[:, 2 * k:2 * k + 2, :], ALU.add).then_inc(mid_sum, 1)
                v.wait_ge(mid_sum, 2 * g + 2)
                for j in range(GT):
                    ins = nc.vector.bn_stats(stat[0][:, j, :], mid[:, j, :])
                ins.then_inc(n1_own, 1)
                v.wait_ge(n1_own, (LN_STEPS + 1) * g + 1)
                inverse_deviation(nc, v, n1_own, (LN_STEPS + 1) * g + 1, stat[0], tmp[0], tmpi[0], rstd[0][:, :], nbias[0][:, :])

            def scale_mid(i, b):
                g = 2 * i + b
                v.wait_ge(z1_ready, g + 1)
                if not (isinstance(i, int) and i == 0):
                    v.wait_ge(fin_sum, 2 * (g - 1))
                nc.vector.tensor_tensor(res2[b][:, :, :], mid[:, :, :], vec[:, G1, :].unsqueeze(1).broadcast_to([P, GT, FEAT]),
                                        ALU.mult).then_inc(mid_scaled, 1)

            def mid_low(i, b):
                g = 2 * i + b
                for k in range(KH):
                    v.wait_ge(ot_hi, KH * g + k + 1)
                    nc.vector.tensor_tensor(ot[1][:, k, :], tp[k][:, :], ot[0][:, k, :].bitcast(fp32), ALU.subtract).then_inc(ot_lo, 1)

            def sum_fin(ip, bp, gp):
                v.wait_ge(res2_ready, gp + 1)
                v.wait_ge(stored[bp], 16 * (ip + 1))
                for k in range(2):
                    v.wait_ge(ffn_done, 2 * gp + k + 1)
                    nc.vector.tensor_tensor(fin[bp][:, 2 * k:2 * k + 2, :], yp[k][:, :, :], res2[bp][:, 2 * k:2 * k + 2, :], ALU.add).then_inc(fin_sum, 1)

            def finish_group(ip, bp, gp):
                v.wait_ge(fin_sum, 2 * gp + 2)
                for j in range(GT):
                    ins = nc.vector.bn_stats(stat[1][:, j, :], fin[bp][:, j, :])
                ins.then_inc(n2_own, 1)
                c = (LN_STEPS + 2) * gp
                v.wait_ge(n2_own, c + 1)
                inverse_deviation(nc, v, n2_own, c + 1, stat[1], tmp[1], tmpi[1], rstd[1][:, :], nbias[1][:, :])
                v.wait_ge(z2_ready, gp + 1)
                nc.vector.tensor_tensor(fin[bp][:, :, :], fin[bp][:, :, :], vec[:, G2, :].unsqueeze(1).broadcast_to([P, GT, FEAT]),
                                        ALU.mult).then_inc(n2_own, 1)
                v.wait_ge(n2_own, c + LN_STEPS + 2)
                v.wait_ge(xb_ready, gp + 1)
                nc.vector.tensor_tensor(fin[bp][:, :, :], fin[bp][:, :, :], xb[bp][:, :, :], ALU.add).then_inc(fin_ready, 1)

            nc.vector.memset(same[:, 0:1], 0.0)
            nc.vector.memset(tin[:, 3, :, :], 0.0)
            nc.vector.memset(tback[:, :, :], 0.0)
            nc.vector.tensor_copy(isrc[:, :], idx_src[:, 0:SGT])
            nc.vector.tensor_copy(idst[:, :], idx_dst[:, 0:SGT])
            nc.vector.memset(same[:, P:P + 1], 0.0).then_inc(cleared, 1)
            v.wait_ge(cleared, 2)
            stage_norm(0, 0)
            att_scores(0)
            att_max(0)
            att_weights(0)
            att_messages(0)
            att_own_weights(0)

            def body(i):
                for b in range(2):
                    ip, bp, gp = before(i, b)
                    if b == 0:
                        stage_norm(i, 1)
                    elif not is_last(i):
                        stage_norm(i + 1, 0)
                    attend = b == 1 and not is_last(i)
                    sum_agg(i, b)
                    agg_low(i, b)
                    if attend:
                        att_max(i + 1)
                    sum_mid(i, b)
                    if attend:
                        att_weights(i + 1)
                    scale_mid(i, b)
                    if attend:
                        att_messages(i + 1)
                    if not is_first(i, b):
                        sum_fin(ip, bp, gp)
                    mid_low(i, b)
                    if not is_first(i, b):
                        finish_group(ip, bp, gp)
                    if b == 0 and not is_last(i):
                        att_scores(i + 1)
                    if attend:
                        att_own_weights(i + 1)

            every(v, body)
            sum_fin(SG - 1, 1, 2 * SG - 1)
            finish_group(SG - 1, 1, 2 * SG - 1)

        @block.tensor
        def _(pe):
            def product(out_ap, pairs):
                n = 0
                for lhs, rhs in pairs:
                    for a, c in ((0, 0), (0, 1), (1, 0)):
                        mm = nc.tensor.matmul(out_ap, lhs[a], rhs[c], start=n == 0, stop=n == 3 * len(pairs) - 1)
                        n += 1
                return mm

            def turn_scores(i):
                pe.wait_ge(tin_ready, i + 1)
                if not is_first(i):
                    pe.wait_ge(pself_ready, i)
                for k in range(3):
                    tr = nc.tensor.transpose(ap[:, k * P:(k + 1) * P], tin[:, k:k + 2, :, :].rearrange("p k t h -> p (k t h)"), ident[:, :])
                tr.then_inc(tin_turned, 1)

            def turn_weights(i):
                pe.wait_ge(tback_ready, i + 1)
                for k in range(3):
                    tr = nc.tensor.transpose(ap[:, k * SH:k * SH + P], tback[:, k, :], ident[:, :])
                tr.then_inc(tback_turned, 1)

            def select_loops(i):
                pe.wait_ge(msg_ready, i + 1)
                for t in range(SGT):
                    mm = nc.tensor.matmul(ap[:, 256 + 16 * t:272 + 16 * t], hot[:, t, :],
                                          sel[:, t, :, :].rearrange("p s h -> p (s h)"), start=True, stop=True)
                mm.then_inc(sel_turned, 1)

            def segments(i, b):
                g = 2 * i + b
                pe.wait_ge(msg_ready, i + 1)
                for j in range(GT):
                    if j % 2 == 0 and not is_first(i, b):
                        pe.wait_ge(mid_sum, 2 * (g - 1) + j // 2 + 1)
                    mm = nc.tensor.matmul(segp[j // 2][:, j % 2, :], hot[:, GT * b + j, :], msg[:, GT * b + j, :], start=True, stop=True)
                    if j % 2:
                        mm.then_inc(seg_done, 1)

            def turn_agg(i, b):
                g = 2 * i + b
                pe.wait_ge(agg_ready, 2 * g + 2)
                if not is_first(i, b):
                    pe.wait_ge(gelu_done, HM * g - 1)
                for k in range(KH):
                    for j in range(GT):
                        tr = nc.tensor.transpose(tp[k][:, j * P:(j + 1) * P], agg[:, j, k * P:(k + 1) * P], ident[:, :])
                    tr.then_inc(agg_turned, 1)

            def project_out(i, b):
                g = 2 * i + b
                pe.wait_ge(at_lo, KH * (g + 1))
                for j in range(GT):
                    mm = product(segp[j // 2][:, j % 2, :],
                                 [([at[a][:, k, j * P:(j + 1) * P] for a in range(2)], [wo[a][:, k, :] for a in range(2)]) for k in range(KH)])
                    if j % 2:
                        mm.then_inc(wo_done, 1)

            def turn_mid(i, b):
                g = 2 * i + b
                pe.wait_ge(z1_ready, g + 1)
                for k in range(KH):
                    pe.wait_ge(at_lo, KH * g + k + 1)
                    for j in range(GT):
                        tr = nc.tensor.transpose(tp[k][:, j * P:(j + 1) * P], mid[:, j, k * P:(k + 1) * P], ident[:, :])
                    tr.then_inc(mid_turned, 1)

            def hidden(gp, first):
                pe.wait_ge(ot_lo, KH * (gp + 1))
                for m in range(HM):
                    if m == 3:
                        pe.wait_ge(gelu_done, HM * gp + 1)
                    elif m == 0 and not first:
                        pe.wait_ge(gelu_done, HM * gp)
                    product(chunk_bank[m][:, :],
                            [([w1[a][:, k, m * P:(m + 1) * P] for a in range(2)], [ot[a][:, k, :] for a in range(2)])
                             for k in range(KH)]).then_inc(chunk_done, 1)

            def feed(gp, tiles, first=False):
                for j in tiles:
                    if j == 0:
                        pe.wait_ge(gelu_done, HM * (gp + 1))
                    if j % 2 == 0 and not first:
                        pe.wait_ge(fin_sum, 2 * (gp - 1) + j // 2 + 1)
                    for m in range(HM):
                        mm = nc.tensor.matmul(yp[j // 2][:, j % 2, :], hid[:, m, j * P:(j + 1) * P], w2[:, m, :],
                                              start=m == 0, stop=m == HM - 1)
                    if j % 2:
                        mm.then_inc(ffn_done, 1)

            turn_scores(0)
            turn_weights(0)
            select_loops(0)

            def body(i):
                for b in range(2):
                    ip, bp, gp = before(i, b)
                    attend = b == 1 and not is_last(i)
                    segments(i, b)
                    if not is_first(i, b):
                        hidden(gp, is_first(i))
                    if attend:
                        turn_scores(i + 1)
                    turn_agg(i, b)
                    if not is_first(i, b):
                        feed(gp, (0,), is_first(i))
                    project_out(i, b)
                    if not is_first(i, b):
                        feed(gp, (1, 2), is_first(i))
                    if attend:
                        turn_weights(i + 1)
                    if not is_first(i, b):
                        feed(gp, (3,))
                    turn_mid(i, b)
                    if attend:
                        select_loops(i + 1)

            every(pe, body)
            hidden(2 * SG - 1, False)
            feed(2 * SG - 1, range(GT))


_INS = ["x", "src", "dst", "L0_gnn_Wq", "L0_gnn_Wk", "L0_gnn_Wv", "L0_gnn_Wo_w", "L0_gnn_Wo_b", "L0_gnn_ln1_g",
        "L0_gnn_ln1_b", "L0_gnn_ln2_g", "L0_gnn_ln2_b", "L0_gnn_ffn_w1", "L0_gnn_ffn_b1", "L0_gnn_ffn_w2", "L0_gnn_ffn_b2"]


def kernel(**inputs):
    import numpy as np
    import concourse.bacc as bacc
    from concourse import mybir
    from concourse.bass_utils import run_bass_kernel_spmd

    nc = bacc.Bacc("TRN2", target_bir_lowering=False, num_devices=1)
    arrays, args = {}, []
    for name in _INS:
        a = np.ascontiguousarray(inputs[name])
        arrays["in_" + name] = a
        args.append(nc.dram_tensor("in_" + name, a.shape, mybir.dt.from_np(a.dtype), kind="ExternalInput").ap())
    shape = arrays["in_x"].shape
    args.append(nc.dram_tensor("out_0", shape, mybir.dt.float32, kind="ExternalOutput").ap())
    program(nc, *args)
    return run_bass_kernel_spmd(nc, [arrays], core_ids=[0]).results[0]["out_0"]
```

```python
from contextlib import ExitStack

import concourse.bass as bass
from concourse import mybir

P = 128
FEAT = 256
HEADS = 8
HEAD = FEAT // HEADS
HID = 512
KH = FEAT // P
HM = HID // P
GT = 4
SGT = 8
SGN = SGT * P
QS = FEAT + HEADS
SCALE = float(HEAD) ** -0.5
EPS = 1e-5
WIN = 3 * P
NO_SLOT = 70000.0
PAD_DST = 200000
PAD_SRC = 100000
HOLE = 0x007FFFFF
PACK = 23

fp32 = mybir.dt.float32
fp32r = mybir.dt.float32r
i32 = mybir.dt.int32
u32 = mybir.dt.uint32
ALU = mybir.AluOpType
ACT = mybir.ActivationFunctionType
AX = mybir.AxisListType.X


def program(nc, x, src, dst, Wq, Wk, Wv, Wo, Wo_b, g1, b1, g2, b2, W1, fb1, W2, fb2, out):
    N = x.shape[0]
    E = src.shape[0]
    SG = -(-N // SGN)
    T = SG * SGT
    T0 = T - SGT
    LAP = SG * SGN - N
    NB = -(-T // P)
    NT = NB * P
    W = E // P + 4
    assert T + SGT <= NT and N < 65535 and N >= SGN and T0 * P < 32768 * 4

    qs_d = nc.dram_tensor("qs_table", [N, QS], fp32).ap()
    kv_d = nc.dram_tensor("kv_table", [N, 2 * FEAT], fp32).ap()
    ep_src = nc.dram_tensor("edges_src", [(W + 1) * P], i32).ap()
    ep_dst = nc.dram_tensor("edges_dst", [(W + 1) * P], i32).ap()
    agg_d = nc.dram_tensor("general_agg", [N, FEAT], fp32).ap()

    outer = ExitStack()
    with outer:
        keep = lambda n, s, d=fp32: outer.enter_context(nc.sbuf_tensor(n, s, d))
        ident = keep("ident", [P, P])
        colf = keep("colf", [P, P])
        idx_src = keep("idx_src", [P, NT], u32)
        idx_dst = keep("idx_dst", [P, NT], u32)
        slot_dst = keep("slot_dst", [P, NT])
        tile_row = keep("tile_row", [P, NT])
        sself = keep("sself", [P, T, HEADS])
        rstd_all = keep("rstd_all", [P, T])
        nbias_all = keep("nbias_all", [P, T])
        flag = keep("flag", [1, 1], i32)
        wo = keep("wo", [P, KH, FEAT])
        w1 = [keep(f"w1{k}", [P, KH, HID], fp32r) for k in range(2)]
        w2 = keep("w2", [P, HM, FEAT])
        vec = keep("vec", [P, 6, FEAT])
        brow = keep("bias_rows", [64, 2, FEAT], fp32r)
        pick = keep("pick", [64, P], fp32r)
        hb1 = keep("hb1", [P, HM])
        b1col = keep("b1col", [P, KH])

        with ExitStack() as early:
            wqkv = [early.enter_context(nc.sbuf_tensor(f"wqkv{k}", [P, KH, 3 * FEAT], fp32r)) for k in range(2)]
            prepare(nc, locals())
            project(nc, locals())
        general(nc, locals())
        finish(nc, locals())


def tensors(nc, stack):
    return (lambda n, s, d=fp32: stack.enter_context(nc.sbuf_tensor(n, s, d)),
            lambda n, s, d=fp32: stack.enter_context(nc.psum_tensor(n, s, d)),
            lambda n: stack.enter_context(nc.semaphore(n)))


def prepare(nc, env):
    (x, src, dst, ident, colf, idx_src, idx_dst, slot_dst, flag, vec, hb1, b1col, ep_src, ep_dst, brow, pick) = (
        env[k] for k in "x src dst ident colf idx_src idx_dst slot_dst flag vec hb1 b1col ep_src ep_dst brow pick".split())
    N, E, T, T0, LAP, NB, NT, W = (env[k] for k in "N E T T0 LAP NB NT W".split())
    PADS = (W + 1) * P - E
    SPLIT = next(d for d in range(16, 0, -1) if E % d == 0)
    weights = [(env["Wq"], env["wqkv"], 0, FEAT), (env["Wk"], env["wqkv"], FEAT, FEAT),
               (env["Wv"], env["wqkv"], 2 * FEAT, FEAT),
               (env["W1"], env["w1"], 0, HID)]
    with ExitStack() as stack:
        sb, ps, sem = tensors(nc, stack)
        brow_hi = sb("bias_high", [64, 2, FEAT], fp32r)
        raw = [sb(f"raw{i}", [P, w.shape[0] // P, w.shape[1]]) for i, (w, _, _, _) in enumerate(weights)]
        padd = sb("padd", [1, PADS], i32)
        pads = sb("pads", [1, PADS], i32)
        coli = sb("coli", [P, P], i32)
        rowi = sb("rowi", [P, NT], i32)
        bpi = sb("bpi", [P, NB], i32)
        posi = sb("posi", [P, WIN], i32)
        rowf = env["tile_row"]
        rowl = sb("rowl", [P, NT])
        bp = sb("bp", [P, 2, NB])
        bpl = sb("bpl", [P, NB])
        posf = sb("posf", [P, WIN])
        ones = sb("ones", [P, P])
        de = sb("de", [P, W], i32)
        dn = sb("dn", [P, W], i32)
        se = sb("se", [P, W], i32)
        ta = sb("ta", [P, W])
        tb = sb("tb", [P, W])
        sums = sb("sums", [P, 3])
        cmpm = sb("cmpm", [P, 2, NT])
        first = sb("first", [P, 1])
        coarse = sb("coarse", [P, 2 * NB])
        crow = sb("crow", [P, 2 * NB], u32)
        rowbuf = sb("rowbuf", [P, 2, W], i32)
        start = sb("start", [P, 2, NB])
        cnt = sb("cnt", [P, 2 * NB])
        st_i = sb("st_i", [P, NB], i32)
        c0 = sb("c0", [P, 3, NB], i32)
        c0f = sb("c0f", [P, NB])
        c0u = sb("c0u", [P, 3, NB], u32)
        off = sb("off", [P, NB])
        wsrc = sb("wsrc", [P, NB, WIN], i32)
        wdst = sb("wdst", [P, NB, WIN], i32)
        dl = sb("dl", [P, NB, WIN])
        va = sb("va", [P, NB, WIN])
        vb = sb("vb", [P, NB, WIN])
        mi = sb("mi", [P, NB, WIN], i32)
        vi = sb("vi", [P, NB, WIN], i32)
        vo = sb("vo", [P, NB, WIN], i32)
        hole = sb("hole", [P, NB, WIN], i32)
        tot = sb("tot", [1, 4])
        g1col = sb("g1col", [P, KH])
        bias_ready = sem("hidden_bias_ready")
        pc = ps("pc", [P, 512])
        pb = ps("pb", [P, 512])
        pt = [ps("pt0", [P, 512]), ps("pt1", [P, 512])]
        loaded = sem("weights_loaded")
        vecs = sem("vectors_loaded")
        consts = sem("constants_made")
        wiped = sem("windows_wiped")
        padded = sem("edges_padded")
        edges = sem("edges_loaded")
        own = sem("dve_own")
        cmp_ready = sem("compare_ready")
        coarse_ready = sem("coarse_ready")
        crow_ready = sem("coarse_row_ready")
        row_loaded = [sem("row_loaded0"), sem("row_loaded1")]
        row_used = sem("row_used")
        c0_ready = sem("window_row_ready")
        win_loaded = sem("window_loaded")
        sums_ready = sem("sums_ready")
        tot_ready = sem("totals_ready")
        slots_ready = sem("slots_ready")
        slots_turned = sem("slots_turned")
        block = stack.enter_context(nc.Block())

        @block.sync
        def _(sp):
            sp.dma_start(ep_dst[0:E].rearrange("(a b) -> a b", a=SPLIT), dst.rearrange("(a b) -> a b", a=SPLIT)).then_inc(padded, 16)
            sp.dma_start(ep_src[0:E].rearrange("(a b) -> a b", a=SPLIT), src.rearrange("(a b) -> a b", a=SPLIT)).then_inc(padded, 16)
            sp.wait_ge(consts, 1)
            sp.dma_start(ep_dst[E:(W + 1) * P].rearrange("(a b) -> a b", a=1), padd[:, :]).then_inc(padded, 16)
            sp.dma_start(ep_src[E:(W + 1) * P].rearrange("(a b) -> a b", a=1), pads[:, :]).then_inc(padded, 16)
            sp.wait_ge(padded, 64)
            sp.dma_start(de[:, :], ep_dst[0:W * P].rearrange("(p c) -> p c", p=P)).then_inc(edges, 16)
            sp.dma_start(dn[:, :], ep_dst[1:W * P + 1].rearrange("(p c) -> p c", p=P)).then_inc(edges, 16)
            sp.dma_start(se[:, :], ep_src[0:W * P].rearrange("(p c) -> p c", p=P)).then_inc(edges, 16)

        @block.scalar
        def _(act):
            for i, (w, _, _, _) in enumerate(weights):
                act.dma_start(raw[i][:, :, :], w.rearrange("(k p) n -> p k n", p=P)).then_inc(loaded, 16)
            act.dma_start(env["wo"][:, :, :], env["Wo"].rearrange("(k p) n -> p k n", p=P)).then_inc(loaded, 16)
            act.dma_start(env["w2"][:, :, :], env["W2"].rearrange("(k p) n -> p k n", p=P)).then_inc(loaded, 16)
            for i, v in enumerate([env["Wo_b"], env["g1"], env["b1"], env["g2"], env["b2"], env["fb2"]]):
                act.dma_start(vec[:, i, :], v.partition_broadcast(P)).then_inc(vecs, 16)
            act.dma_start(hb1[:, :], env["fb1"].rearrange("(m p) -> p m", p=P), allow_slow_non_contiguous=True).then_inc(vecs, 16)
            act.dma_start(b1col[:, :], env["b1"].rearrange("(m p) -> p m", p=P), allow_slow_non_contiguous=True).then_inc(vecs, 16)
            act.dma_start(g1col[:, :], env["g1"].rearrange("(m p) -> p m", p=P), allow_slow_non_contiguous=True).then_inc(vecs, 16)
            act.wait_ge(vecs, 16 * 9)

        @block.gpsimd
        def _(pool):
            nc.gpsimd.memset(padd[:, :], PAD_DST)
            nc.gpsimd.memset(pads[:, :], PAD_SRC).then_inc(consts, 1)
            nc.gpsimd.memset(ident[:, :], 0.0)
            nc.gpsimd.memset(ones[:, :], 1.0)
            nc.gpsimd.iota(coli[:, :], [[1, P]], base=0, channel_multiplier=0)
            nc.gpsimd.iota(rowi[:, :], [[P, NT]], base=0, channel_multiplier=0)
            nc.gpsimd.iota(bpi[:, :], [[P * P, NB]], base=0, channel_multiplier=P)
            nc.gpsimd.iota(posi[:, :], [[1, WIN]], base=0, channel_multiplier=0).then_inc(consts, 1)
            pool.wait_ge(consts, 2)
            nc.gpsimd.affine_select(out=ident[:, :], in_=ident[:, :], compare_op=ALU.not_equal, fill=1.0,
                                    base=0, pattern=[[-1, P]], channel_multiplier=1).then_inc(consts, 1)
            nc.gpsimd.memset(wsrc[:, :, :], 0)
            nc.gpsimd.memset(wdst[:, :, :], 0).then_inc(wiped, 1)
            pool.wait_ge(crow_ready, 1)
            pool.wait_ge(padded, 64)
            for k in range(2 * NB):
                if k >= 2:
                    pool.wait_ge(row_used, k - 1)
                nc.gpsimd.indirect_dma_start(
                    out=rowbuf[:, k % 2, :], out_offset=None, in_=ep_dst[0:W * P].rearrange("(p c) -> p c", p=P),
                    in_offset=bass.IndirectOffsetOnAxis(ap=crow[:, k:k + 1], axis=0)).then_inc(row_loaded[k % 2], 16)
            pool.wait_ge(c0_ready, 1)
            pool.wait_ge(wiped, 1)
            for k in range(NB):
                for r in range(3):
                    for buf, tab in ((wsrc, ep_src), (wdst, ep_dst)):
                        nc.gpsimd.indirect_dma_start(
                            out=buf[:, k, r * P:(r + 1) * P], out_offset=None,
                            in_=tab.rearrange("(r c) -> r c", c=P),
                            in_offset=bass.IndirectOffsetOnAxis(ap=c0u[:, r, k:k + 1], axis=0),
                            bounds_check=W, oob_is_err=False).then_inc(win_loaded, 16)

        @block.tensor
        def _(pe):
            pe.wait_ge(cmp_ready, 1)
            pe.wait_ge(consts, 2)
            for h in range(2):
                for k in range(NB):
                    c = h * NB + k
                    mm = nc.tensor.matmul(pc[:, c:c + 1], cmpm[:, h, k * P:(k + 1) * P], ones[:, 0:1], start=True, stop=True)
            mm.then_inc(coarse_ready, 1)
            pe.wait_ge(loaded, 16 * (len(weights) + 2))
            pe.wait_ge(vecs, 16 * 9)
            for m in range(HM):
                for k in range(KH):
                    mm = nc.tensor.matmul(pb[:, m:m + 1], raw[3][:, k, m * P:(m + 1) * P], b1col[:, k:k + 1],
                                          start=k == 0, stop=k == KH - 1)
            mm.then_inc(bias_ready, 1)
            pe.wait_ge(sums_ready, 1)
            nc.tensor.matmul(pc[:, 64:67], ones[:, :], sums[:, :], start=True, stop=True).then_inc(tot_ready, 1)
            pe.wait_ge(slots_ready, 1)
            pe.wait_ge(consts, 3)
            for q, buf in enumerate((va, vb)):
                for k in range(NB):
                    tr = nc.tensor.transpose(pt[q][:, k * P:(k + 1) * P], buf[:, k, 0:P], ident[:, :])
            tr.then_inc(slots_turned, 1)

        @block.vector
        def _(v):
            done = [0]

            def seq(ins):
                done[0] += 1
                ins.then_inc(own, 1)
                v.wait_ge(own, done[0])

            v.wait_ge(consts, 2)
            seq(nc.vector.tensor_copy(colf[:, :], coli[:, :]))
            seq(nc.vector.tensor_copy(posf[:, :], posi[:, :]))
            seq(nc.vector.tensor_copy(rowf[:, :], rowi[:, :]))
            seq(nc.vector.tensor_copy(bp[:, 0, :], bpi[:, :]))
            seq(nc.vector.tensor_scalar(rowl[:, :], rowf[:, :], float(P * T0), float(-LAP), ALU.is_ge, ALU.mult))
            seq(nc.vector.tensor_tensor(rowf[:, :], rowf[:, :], rowl[:, :], ALU.add))
            seq(nc.vector.tensor_scalar(bpl[:, :], bp[:, 0, :], float(P * T0), float(-LAP), ALU.is_ge, ALU.mult))
            seq(nc.vector.tensor_tensor(bp[:, 0, :], bp[:, 0, :], bpl[:, :], ALU.add))
            seq(nc.vector.tensor_scalar(bp[:, 1, :], bp[:, 0, :], float(P), None, ALU.add))
            seq(nc.vector.memset(hole[:, :, :], HOLE))
            v.wait_ge(edges, 48)
            seq(nc.vector.tensor_copy(first[:, :], de[:, 0:1]))
            seq(nc.vector.tensor_scalar(cmpm[:, 0, :], rowf[:, :], first[:, 0:1], None, ALU.is_gt))
            seq(nc.vector.tensor_scalar(rowl[:, :], rowf[:, :], float(P), None, ALU.add))
            nc.vector.tensor_scalar(cmpm[:, 1, :], rowl[:, :], first[:, 0:1], None, ALU.is_gt).then_inc(cmp_ready, 1)
            seq(nc.vector.tensor_tensor(ta[:, :], dn[:, :], de[:, :], ALU.is_ge))
            seq(nc.vector.tensor_reduce(sums[:, 0:1], ta[:, :], AX, ALU.add))
            seq(nc.vector.tensor_tensor(ta[:, :], dn[:, :], de[:, :], ALU.not_equal))
            seq(nc.vector.tensor_tensor(tb[:, :], se[:, :], de[:, :], ALU.is_equal))
            seq(nc.vector.tensor_tensor(ta[:, :], ta[:, :], tb[:, :], ALU.mult))
            seq(nc.vector.tensor_reduce(sums[:, 1:2], ta[:, :], AX, ALU.add))
            v.wait_ge(coarse_ready, 1)
            seq(nc.vector.tensor_scalar(coarse[:, :], pc[:, 0:2 * NB], -1.0, 0.0, ALU.add, ALU.max))
            nc.vector.tensor_copy(crow[:, :], coarse[:, :]).then_inc(crow_ready, 1)
            for k in range(2 * NB):
                v.wait_ge(row_loaded[k % 2], 16 * (k // 2 + 1))
                seq(nc.vector.tensor_scalar(ta[:, :], rowbuf[:, k % 2, :], bp[:, k // NB, k % NB:k % NB + 1], None, ALU.is_lt))
                nc.vector.tensor_reduce(cnt[:, k:k + 1], ta[:, :], AX, ALU.add).then_inc(row_used, 1)
                v.wait_ge(row_used, k + 1)
            seq(nc.vector.scalar_tensor_tensor(start[:, :, :].rearrange("p a b -> p (a b)"), coarse[:, :], float(W),
                                               cnt[:, :], ALU.mult, ALU.add))
            seq(nc.vector.tensor_copy(st_i[:, :], start[:, 0, :]))
            seq(nc.vector.tensor_scalar(c0[:, 0, :], st_i[:, :], 7, None, ALU.logical_shift_right))
            seq(nc.vector.tensor_copy(c0f[:, :], c0[:, 0, :]))
            for r in range(3):
                ins = nc.vector.tensor_scalar(c0u[:, r, :], c0f[:, :], float(r), None, ALU.add)
            ins.then_inc(c0_ready, 1)
            seq(nc.vector.scalar_tensor_tensor(off[:, :], c0f[:, :], float(-P), start[:, 0, :], ALU.mult, ALU.add))
            seq(nc.vector.tensor_tensor(cnt[:, 0:NB], start[:, 1, :], start[:, 0, :], ALU.subtract))
            seq(nc.vector.tensor_scalar(cnt[:, 0:NB], cnt[:, 0:NB], float(2 * P), None, ALU.is_gt))
            nc.vector.tensor_reduce(sums[:, 2:3], cnt[:, 0:NB], AX, ALU.add).then_inc(sums_ready, 1)
            v.wait_ge(tot_ready, 1)
            seq(nc.vector.tensor_scalar(tot[:, 0:1], pc[0:1, 64:65], float(P * W), None, ALU.is_equal))
            seq(nc.vector.tensor_scalar(tot[:, 1:2], pc[0:1, 65:66], float(N), None, ALU.is_equal))
            seq(nc.vector.tensor_scalar(tot[:, 2:3], pc[0:1, 66:67], 0.0, None, ALU.is_equal))
            seq(nc.vector.tensor_tensor(tot[:, 0:1], tot[:, 0:1], tot[:, 1:2], ALU.mult))
            seq(nc.vector.tensor_tensor(tot[:, 0:1], tot[:, 0:1], tot[:, 2:3], ALU.mult))
            seq(nc.vector.tensor_scalar(flag[:, :], tot[:, 0:1], -1.0, 1.0, ALU.mult, ALU.add))
            v.wait_ge(vecs, 16 * 9)
            seq(nc.vector.tensor_tensor(vec[:, 5, :], vec[:, 5, :], vec[:, 2, :], ALU.add))
            seq(nc.vector.memset(brow[:, :, :].bitcast(fp32), 0.0))
            seq(nc.vector.tensor_copy(pick[:, :], ones[0:64, :]))
            for r, k in enumerate((0, 5)):
                seq(nc.vector.tensor_copy(brow_hi[:, r, :], vec[0:64, k, :]))
                seq(nc.vector.tensor_copy(brow[0:1, r, :], vec[0:1, k, :]))
                seq(nc.vector.tensor_tensor(brow[32:33, r, :], vec[32:33, k, :], brow_hi[32:33, r, :].bitcast(fp32), ALU.subtract))
            v.wait_ge(loaded, 16 * (len(weights) + 2))
            v.wait_ge(bias_ready, 1)
            seq(nc.vector.tensor_tensor(hb1[:, :], hb1[:, :], pb[:, 0:HM], ALU.add))
            for k in range(KH):
                seq(nc.vector.tensor_scalar(raw[3][:, k, :], raw[3][:, k, :], g1col[:, k:k + 1], None, ALU.mult))
            for i, (_, parts, c, n) in enumerate(weights):
                seq(nc.vector.tensor_copy(parts[0][:, :, c:c + n], raw[i][:, :, :]))
                seq(nc.vector.tensor_tensor(parts[1][:, :, c:c + n], raw[i][:, :, :], parts[0][:, :, c:c + n].bitcast(fp32), ALU.subtract))
            v.wait_ge(win_loaded, 16 * 6 * NB)
            seq(nc.vector.tensor_tensor(dl[:, :, :], wdst[:, :, :], bp[:, 0, :].unsqueeze(2).broadcast_to([P, NB, WIN]), ALU.subtract))
            seq(nc.vector.memset(va[:, :, WIN - 1:WIN], 0.0))
            seq(nc.vector.tensor_tensor(va[:, :, 0:WIN - 1], wdst[:, :, 0:WIN - 1], wdst[:, :, 1:WIN], ALU.not_equal))
            seq(nc.vector.tensor_tensor(vb[:, :, :], wsrc[:, :, :], wdst[:, :, :], ALU.is_equal))
            seq(nc.vector.tensor_tensor(va[:, :, :], va[:, :, :], vb[:, :, :], ALU.mult))
            seq(nc.vector.tensor_scalar(vb[:, :, :], dl[:, :, :], 0.0, None, ALU.is_ge))
            seq(nc.vector.scalar_tensor_tensor(vb[:, :, :].rearrange("p k c -> p (k c)"), dl[:, :, :].rearrange("p k c -> p (k c)"), float(P),
                                               vb[:, :, :].rearrange("p k c -> p (k c)"), ALU.is_lt, ALU.mult))
            seq(nc.vector.tensor_scalar(va[:, :, :], va[:, :, :], -1.0, 1.0, ALU.mult, ALU.add))
            seq(nc.vector.tensor_tensor(va[:, :, :], va[:, :, :], vb[:, :, :], ALU.mult))
            seq(nc.vector.tensor_scalar(mi[:, :, :], va[:, :, :], -1.0, 1.0, ALU.mult, ALU.add))
            seq(nc.vector.tensor_tensor(vb[:, :, :], dl[:, :, :], off[:, :].unsqueeze(2).broadcast_to([P, NB, WIN]), ALU.add))
            seq(nc.vector.tensor_copy(vo[:, :, :], vb[:, :, :]))
            seq(nc.vector.tensor_scalar(vo[:, :, :], vo[:, :, :], PACK, None, ALU.logical_shift_left))
            seq(nc.vector.tensor_copy(vi[:, :, :], dl[:, :, :]))
            seq(nc.vector.tensor_tensor(vi[:, :, :], vi[:, :, :], vo[:, :, :], ALU.bitwise_or))
            seq(nc.vector.tensor_scalar(vo[:, :, :], wsrc[:, :, :], 7, None, ALU.logical_shift_left))
            seq(nc.vector.tensor_tensor(vi[:, :, :], vi[:, :, :], vo[:, :, :], ALU.bitwise_or))
            seq(nc.vector.copy_predicated(vi[:, :, :], mi[:, :, :], hole[:, :, :]))
            for b in range(8):
                d = 1 << b
                seq(nc.vector.tensor_scalar(mi[:, :, :], vi[:, :, :], PACK + b, 1, ALU.logical_shift_right, ALU.bitwise_and))
                seq(nc.vector.tensor_copy(vo[:, :, :], vi[:, :, :]))
                seq(nc.vector.copy_predicated(vi[:, :, :], mi[:, :, :], hole[:, :, :]))
                seq(nc.vector.copy_predicated(vi[:, :, 0:WIN - d], mi[:, :, d:WIN], vo[:, :, d:WIN]))
            seq(nc.vector.tensor_scalar(mi[:, :, 0:P], vi[:, :, 0:P], 7, 0xFFFF, ALU.logical_shift_right, ALU.bitwise_and))
            seq(nc.vector.tensor_copy(va[:, :, 0:P], mi[:, :, 0:P]))
            seq(nc.vector.tensor_scalar(vo[:, :, 0:P], vi[:, :, 0:P], 127, None, ALU.bitwise_and))
            seq(nc.vector.tensor_copy(dl[:, :, 0:P], vo[:, :, 0:P]))
            seq(nc.vector.tensor_scalar(vb[:, :, 0:P], va[:, :, 0:P], 65535.0, NO_SLOT, ALU.is_equal, ALU.mult))
            nc.vector.tensor_tensor(vb[:, :, 0:P], vb[:, :, 0:P], dl[:, :, 0:P], ALU.add).then_inc(slots_ready, 1)
            v.wait_ge(slots_turned, 1)
            nc.vector.tensor_copy(idx_src[:, :], pt[0][:, 0:NT])
            seq(nc.vector.tensor_copy(slot_dst[:, :], pt[1][:, 0:NT]))
            seq(nc.vector.tensor_tensor(idx_dst[:, :], slot_dst[:, :], rowf[:, :], ALU.add))


RSQRT_SEED = float(0x5F1FFFF9)
SEED_A, SEED_B = 0.703952253, 2.38924456
LN_STEPS = 16
LN_CHAIN = 7


def inverse_deviation(nc, v, own, base, stat, tmp, tmpi, rstd, nbias, meanwhile=None):
    mean_e, m2_e, mean_o, m2_o = (stat[:, :, k] for k in (1, 2, 4, 5))
    total, diff, var, root, corr = (tmp[:, k, :] for k in range(5))

    def behind(step):
        if meanwhile:
            meanwhile(step)

    nc.vector.tensor_tensor(diff, mean_e, mean_o, ALU.subtract).then_inc(own, 1)
    nc.vector.tensor_tensor(var, m2_e, m2_o, ALU.add).then_inc(own, 1)
    nc.vector.tensor_tensor(total, mean_e, mean_o, ALU.add).then_inc(own, 1)
    v.wait_ge(own, base + 2)
    nc.vector.scalar_tensor_tensor(diff, diff, 0.25, diff, ALU.mult, ALU.mult).then_inc(own, 1)
    nc.vector.tensor_scalar(var, var, 1.0 / FEAT, EPS, ALU.mult, ALU.add).then_inc(own, 1)
    v.wait_ge(own, base + 5)
    nc.vector.tensor_tensor(var, var, diff, ALU.add).then_inc(own, 1)
    v.wait_ge(own, base + 6)
    nc.vector.tensor_scalar(tmpi, var.bitcast(i32), 1, None, ALU.logical_shift_right).then_inc(own, 1)
    v.wait_ge(own, base + 7)
    nc.vector.tensor_scalar(root.bitcast(i32), tmpi, -1.0, RSQRT_SEED, ALU.mult, ALU.add).then_inc(own, 1)
    v.wait_ge(own, base + 8)
    nc.vector.scalar_tensor_tensor(corr, root, -SEED_A, root, ALU.mult, ALU.mult).then_inc(own, 1)
    behind(0)
    v.wait_ge(own, base + 9)
    nc.vector.tensor_tensor(corr, corr, var, ALU.mult).then_inc(own, 1)
    behind(1)
    v.wait_ge(own, base + 10)
    nc.vector.scalar_tensor_tensor(root, corr, SEED_A * SEED_B, root, ALU.add, ALU.mult).then_inc(own, 1)
    behind(2)
    v.wait_ge(own, base + 11)
    nc.vector.tensor_tensor(corr, root, root, ALU.mult).then_inc(own, 1)
    behind(3)
    v.wait_ge(own, base + 12)
    nc.vector.tensor_tensor(corr, corr, var, ALU.mult).then_inc(own, 1)
    nc.vector.tensor_scalar(root, root, 0.375, None, ALU.mult)
    behind(4)
    v.wait_ge(own, base + 13)
    nc.vector.scalar_tensor_tensor(corr, corr, -10.0 / 3.0, corr, ALU.add, ALU.mult).then_inc(own, 1)
    behind(5)
    v.wait_ge(own, base + 14)
    nc.vector.scalar_tensor_tensor(rstd, corr, 5.0, root, ALU.add, ALU.mult).then_inc(own, 1)
    behind(6)
    v.wait_ge(own, base + 15)
    nc.vector.scalar_tensor_tensor(nbias, total, -0.5, rstd, ALU.mult, ALU.mult).then_inc(own, 1)


def project(nc, env):
    x, qs_d, kv_d, ident, sself, rstd_all, nbias_all, wqkv = (
        env[k] for k in "x qs_d kv_d ident sself rstd_all nbias_all wqkv".split())
    N, SG = env["N"], env["SG"]
    with ExitStack() as stack:
        sb, ps, sem = tensors(nc, stack)
        xg = [sb(f"xg{b}", [P, GT, FEAT]) for b in range(2)]
        hg = [sb(f"hg{b}", [P, GT, FEAT]) for b in range(2)]
        ht = [[sb(f"ht{b}{k}", [P, KH, GT * P], fp32r) for k in range(2)] for b in range(2)]
        qs = [sb(f"qs{b}", [P, GT, QS]) for b in range(2)]
        kv = [sb(f"kv{b}", [P, GT, 2 * FEAT]) for b in range(2)]
        prod = sb("prod", [P, GT, FEAT])
        stat = sb("stat", [P, GT, 6])
        tmp = sb("tmp", [P, 5, GT])
        tmpi = sb("tmpi", [P, GT], i32)
        rstd = [sb(f"rstd{b}", [P, GT]) for b in range(2)]
        nbias = [sb(f"nbias{b}", [P, GT]) for b in range(2)]
        tp = [ps(f"tp{k}", [P, 512]) for k in range(KH)]
        kvp = [ps(f"kvp{j}", [P, 512]) for j in range(GT)]
        qp = [ps(f"qp{j}", [P, 2, FEAT]) for j in range(2)]
        x_loaded = [sem("x_loaded0"), sem("x_loaded1")]
        qs_stored = [sem("qs_stored0"), sem("qs_stored1")]
        kv_stored = [sem("kv_stored0"), sem("kv_stored1")]
        own = sem("norm_steps")
        stats_own = sem("stats_done")
        norm_ready = sem("norm_ready")
        h_ready = sem("h_ready")
        turned = sem("h_turned")
        hi_ready = sem("ht_high_ready")
        lo_ready = sem("ht_low_ready")
        projected = sem("tile_projected")
        q_ready = sem("q_staged")
        kv_ready = sem("kv_staged")
        prod_ready = sem("score_products")
        score_ready = sem("own_scores_ready")
        block = stack.enter_context(nc.Block())
        own_steps = LN_STEPS

        def rows(i, b):
            first = (N - SGN) if isinstance(i, int) and i == SG - 1 else i * SGN
            return bass.ds(first + b * GT * P, GT * P)

        def every(eng, body):
            body(0)
            with eng.Fori(1, SG - 1) as i:
                body(i)
            body(SG - 1)

        @block.sync
        def _(sp):
            def load(i, b):
                if not (isinstance(i, int) and i == 0):
                    sp.wait_ge(h_ready, 2 * i + b - 1)
                sp.dma_start(xg[b][:, :, :], x[rows(i, b), :].rearrange("(j p) c -> p j c", p=P)).then_inc(x_loaded[b], 16)

            def store(i, b):
                sp.wait_ge(score_ready, 2 * i + b + 1)
                sp.dma_start(qs_d[rows(i, b), :].rearrange("(j p) c -> p j c", p=P), qs[b][:, :, :]).then_inc(qs_stored[b], 16)
                sp.wait_ge(kv_ready, GT * (2 * i + b + 1))
                sp.dma_start(kv_d[rows(i, b), :].rearrange("(j p) c -> p j c", p=P), kv[b][:, :, :]).then_inc(kv_stored[b], 16)

            load(0, 0)
            load(0, 1)
            load(1, 0)
            load(1, 1)
            with sp.Fori(0, SG - 3) as i:
                load(i + 2, 0)
                store(i, 0)
                load(i + 2, 1)
                store(i, 1)
            load(SG - 1, 0)
            store(SG - 3, 0)
            load(SG - 1, 1)
            store(SG - 3, 1)
            store(SG - 2, 0)
            store(SG - 2, 1)
            i = SG - 1
            for b in range(2):
                sp.wait_ge(qs_stored[b], 16 * i)
                sp.wait_ge(kv_stored[b], 16 * i)
            store(i, 0)
            store(i, 1)
            for b in range(2):
                sp.wait_ge(qs_stored[b], 16 * SG)
                sp.wait_ge(kv_stored[b], 16 * SG)

        @block.vector
        def _(v):
            def norm(i, b, t):
                g = 2 * i + b
                v.wait_ge(x_loaded[b], 16 * (i + 1))
                for j in range(GT):
                    st = nc.vector.bn_stats(stat[:, j, :], xg[b][:, j, :])
                st.then_inc(stats_own, 1)
                v.wait_ge(stats_own, g + 1)
                if not (isinstance(i, int) and i == 0):
                    v.wait_ge(h_ready, g - 1)
                inverse_deviation(nc, v, own, own_steps * g, stat, tmp, tmpi[:, :], rstd[b][:, :], nbias[b][:, :])
                v.wait_ge(own, own_steps * (g + 1))
                nc.vector.tensor_copy(rstd_all[:, bass.ds(t, GT)], rstd[b][:, :])
                nc.vector.tensor_copy(nbias_all[:, bass.ds(t, GT)], nbias[b][:, :]).then_inc(norm_ready, 1)

            def low(i, b):
                g = 2 * i + b
                for k in range(KH):
                    v.wait_ge(hi_ready, KH * g + k + 1)
                    nc.vector.tensor_tensor(ht[b][1][:, k, :], tp[k][:, :], ht[b][0][:, k, :].bitcast(fp32),
                                            ALU.subtract).then_inc(lo_ready, 1)

            def scores(i, b, t):
                g = 2 * i + b
                v.wait_ge(prod_ready, g + 1)
                nc.vector.tensor_reduce(qs[b][:, :, FEAT:QS], prod[:, :, :].rearrange("p j (h d) -> p j h d", d=HEAD),
                                        AX, ALU.add).then_inc(score_ready, 1)
                v.wait_ge(score_ready, g + 1)
                nc.vector.tensor_copy(sself[:, bass.ds(t, GT), :], qs[b][:, :, FEAT:QS])

            def body(i):
                final = isinstance(i, int) and i == SG - 1
                for b in range(2):
                    if not final:
                        norm(i + 1, b, SGT * (i + 1) + GT * b)
                    if not (final and b == 1):
                        low(*((i, 1) if b == 0 else (i + 1, 0)))
                    if b == 1:
                        scores(i, 0, SGT * i)
                    elif not (isinstance(i, int) and i == 0):
                        scores(i - 1, 1, SGT * i - GT)

            norm(0, 0, 0)
            norm(0, 1, GT)
            low(0, 0)
            every(v, body)
            scores(SG - 1, 1, SGT * (SG - 1) + GT)

        @block.gpsimd
        def _(pool):
            def products(i, b):
                g = 2 * i + b
                pool.wait_ge(q_ready, 2 * (g + 1))
                if not (isinstance(i, int) and i == 0 and b == 0):
                    pool.wait_ge(score_ready, g)
                nc.gpsimd.tensor_tensor(prod[:, :, :], kv[b][:, :, 0:FEAT], qs[b][:, :, 0:FEAT], ALU.mult).then_inc(prod_ready, 1)

            products(0, 0)
            products(0, 1)
            with pool.Fori(1, SG) as i:
                products(i, 0)
                products(i, 1)

        @block.scalar
        def _(act):
            def make_h(i, b):
                g = 2 * i + b
                act.wait_ge(norm_ready, g + 1)
                if not (isinstance(i, int) and i == 0):
                    act.wait_ge(turned, KH * (g - 1))
                for j in range(GT):
                    ins = nc.scalar.activation(hg[b][:, j, :], xg[b][:, j, :], ACT.Relu, bias=nbias[b][:, j:j + 1],
                                               scale=rstd[b][:, j:j + 1])
                ins.then_inc(h_ready, 1)

            def high(i, b):
                g = 2 * i + b
                if not (isinstance(i, int) and i == 0):
                    act.wait_ge(projected, GT * (g - 1))
                for k in range(KH):
                    act.wait_ge(turned, KH * g + k + 1)
                    nc.scalar.activation(ht[b][0][:, k, :], tp[k][:, :], ACT.Copy).then_inc(hi_ready, 1)

            def stage(i, b, tiles):
                g = 2 * i + b
                if not (isinstance(i, int) and i == 0) and tiles[0] == 0:
                    act.wait_ge(qs_stored[b], 16 * i)
                    act.wait_ge(kv_stored[b], 16 * i)
                for j in tiles:
                    act.wait_ge(projected, GT * g + j + 1)
                    nc.scalar.activation(kv[b][:, j, :], kvp[j][:, :], ACT.Copy).then_inc(kv_ready, 1)
                    if j % 2:
                        nc.scalar.activation(qs[b][:, j - 1:j + 1, 0:FEAT], qp[j // 2][:, :, :], ACT.Copy).then_inc(q_ready, 1)

            def body(i):
                final = isinstance(i, int) and i == SG - 1
                for b in range(2):
                    if not (final and b == 1):
                        high(*((i, 1) if b == 0 else (i + 1, 0)))
                    stage(i, b, range(2))
                    if not final:
                        make_h(i + 1, b)
                    stage(i, b, range(2, GT))

            make_h(0, 0)
            make_h(0, 1)
            high(0, 0)
            every(act, body)

        @block.tensor
        def _(pe):
            def turn(i, b):
                g = 2 * i + b
                pe.wait_ge(h_ready, g + 1)
                for k in range(KH):
                    if not (isinstance(i, int) and i == 0 and b == 0):
                        pe.wait_ge(lo_ready, KH * (g - 1) + k + 1)
                    for j in range(GT):
                        tr = nc.tensor.transpose(tp[k][:, j * P:(j + 1) * P], hg[b][:, j, k * P:(k + 1) * P], ident[:, :])
                    tr.then_inc(turned, 1)

            def multiply(i, b):
                g = 2 * i + b
                pe.wait_ge(lo_ready, KH * (g + 1))
                for j in range(GT):
                    if not (isinstance(i, int) and i == 0 and b == 0):
                        pe.wait_ge(kv_ready, GT * (g - 1) + j + 1)
                        if j % 2 == 0:
                            pe.wait_ge(q_ready, 2 * (g - 1) + j // 2 + 1)
                    n = 0
                    for k in range(KH):
                        for a, w in ((0, 0), (0, 1), (1, 0)):
                            lhs = ht[b][a][:, k, j * P:(j + 1) * P]
                            nc.tensor.matmul(qp[j // 2][:, j % 2, :], lhs, wqkv[w][:, k, 0:FEAT], start=n == 0, stop=n == 5)
                            mm = nc.tensor.matmul(kvp[j][:, :], lhs, wqkv[w][:, k, FEAT:3 * FEAT], start=n == 0, stop=n == 5)
                            n += 1
                    mm.then_inc(projected, 1)

            def body(i):
                for b in range(2):
                    if isinstance(i, int) and i == 0 and b == 0:
                        turn(0, 0)
                    nxt = (i, 1) if b == 0 else (i + 1, 0)
                    if not (isinstance(i, int) and i == SG - 1 and b == 1):
                        turn(*nxt)
                    multiply(i, b)

            every(pe, body)


def general(nc, env):
    (ident, colf, tile_row, idx_src, idx_dst, slot_dst, sself, flag, qs_d, kv_d, ep_src, ep_dst, agg_d) = (
        env[k] for k in "ident colf tile_row idx_src idx_dst slot_dst sself flag qs_d kv_d ep_src ep_dst agg_d".split())
    N, E, T, T0, LAP = (env[k] for k in "N E T T0 LAP".split())
    C = -(-E // P)
    with ExitStack() as stack:
        sb, ps, sem = tensors(nc, stack)
        ids = sb("ids", [P, 2], i32)
        idu = sb("idu", [P, 2], u32)
        nought = sb("nought", [P, 2], i32)
        eq = sb("eq", [P, QS])
        ekv = sb("ekv", [P, 2 * FEAT])
        eqk = sb("eqk", [P, FEAT])
        base = sb("base", [P, 1])
        rel = sb("rel", [P, 1])
        score = sb("score", [P, HEADS])
        pos = sb("pos", [P, HEADS])
        ehot = sb("ehot", [P, P])
        spread = sb("spread", [P, HEADS, P])
        peak = sb("peak", [P, HEADS])
        gmax = sb("gmax", [P, HEADS])
        hot_t = sb("hot_t", [P, P])
        below = sb("below", [P, HEADS])
        wm = sb("wm", [P, QS])
        acc = sb("acc", [P, QS])
        inv = sb("inv", [P, HEADS])
        res = sb("res", [P, FEAT])
        spp = stack.enter_context(nc.psum_tensor("spp", [P, HEADS, P], fp32))
        otp = ps("otp", [P, 512])
        mep = ps("mep", [P, 512])
        sump = ps("sump", [P, 512])
        zeroed = sem("rows_zeroed")
        ids_free = sem("ids_free")
        ids_loaded = sem("ids_loaded")
        idu_ready = sem("indices_ready")
        rows_here = sem("rows_here")
        a_own = sem("max_steps")
        b_own = sem("sum_steps")
        spread_ready = sem("spread_ready")
        spread_turned = sem("spread_turned")
        hot_ready = sem("hot_ready")
        hot_turned = sem("hot_turned")
        hot_t_ready = sem("hot_t_ready")
        edge_max = sem("edge_max")
        below_ready = sem("below_ready")
        weight_ready = sem("weight_ready")
        wm_ready = sem("wm_ready")
        summed = sem("chunk_summed")
        tile_own = sem("tile_steps")
        res_ready = sem("tile_result")
        res_stored = sem("tile_stored")
        rewritten = sem("values_rewritten")
        block = stack.enter_context(nc.Block())
        A_STEPS, B_STEPS, TILE_STEPS = 8, 5, 4

        def walk(eng, chunk, before=None, after=None):
            for lo, hi, back in ((0, T0, 0), (T0, T, LAP)):
                with eng.Fori(lo, hi) as t:
                    if before:
                        before(t)
                    for second in (0, 1):
                        with eng.Fori(0, C) as c:
                            chunk(2 * C * t + C * second + c, t, c, second)
                    if after:
                        after(t, P * t - back)

        @block.sync
        def _(sp):
            need = sp.value_load(flag[0:1, 0:1], min_val=0, max_val=1)
            with sp.If(need > 0):
                def chunk(s, t, c, second):
                    sp.wait_ge(ids_free, s + 1)
                    sp.dma_start(ids[:, 0:1], ep_src[bass.ds(P * c, P)].rearrange("(p a) -> p a", a=1)).then_inc(ids_loaded, 16)
                    sp.dma_start(ids[:, 1:2], ep_dst[bass.ds(P * c, P)].rearrange("(p a) -> p a", a=1)).then_inc(ids_loaded, 16)

                def after(t, row):
                    sp.wait_ge(res_stored, 16 * (t + 1))
                    sp.wait_ge(res_ready, t + 1)
                    sp.dma_start(agg_d[bass.ds(row, P), :], res[:, :]).then_inc(res_stored, 16)

                sp.sem_inc(ids_free, 1)
                sp.sem_inc(res_stored, 16)
                walk(sp, chunk, after=after)
                sp.wait_ge(res_stored, 16 * (T + 1))
                sp.dma_start(kv_d[:, FEAT:2 * FEAT], agg_d).then_inc(rewritten, 16)
                sp.wait_ge(rewritten, 16)

        @block.gpsimd
        def _(pool):
            top_row = pool.to_reg(N - 1)
            need = pool.value_load(flag[0:1, 0:1], min_val=0, max_val=1)
            with pool.If(need > 0):
                nc.gpsimd.memset(nought[:, :], 0).then_inc(zeroed, 1)
                nc.gpsimd.memset(eq[:, :], 0.0)
                nc.gpsimd.memset(ekv[:, :], 0.0).then_inc(zeroed, 1)
                pool.wait_ge(zeroed, 2)

                def chunk(s, t, c, second):
                    pool.wait_ge(ids_loaded, 32 * (s + 1))
                    nc.gpsimd.tensor_tensor(idu[:, :], ids[:, :].bitcast(u32), nought[:, :].bitcast(u32), ALU.add).then_inc(idu_ready, 1)
                    pool.wait_ge(zeroed, 2)
                    pool.wait_ge(idu_ready, s + 1)
                    nc.gpsimd.indirect_dma_start(out=eq[:, :], out_offset=None, in_=qs_d,
                                                 in_offset=bass.IndirectOffsetOnAxis(ap=idu[:, 1:2], axis=0),
                                                 bounds_check=top_row, oob_is_err=False).then_inc(rows_here, 16)
                    nc.gpsimd.indirect_dma_start(out=ekv[:, :], out_offset=None, in_=kv_d,
                                                 in_offset=bass.IndirectOffsetOnAxis(ap=idu[:, 0:1], axis=0),
                                                 bounds_check=top_row, oob_is_err=False).then_inc(rows_here, 16)

                walk(pool, chunk)
                nc.gpsimd.memset(sself[:, :, :], 0.0)
                nc.gpsimd.memset(slot_dst[:, :], NO_SLOT)
                nc.gpsimd.memset(idx_src[:, :], int(NO_SLOT))
                nc.gpsimd.memset(idx_dst[:, :], int(NO_SLOT))

        @block.scalar
        def _(act):
            need = act.value_load(flag[0:1, 0:1], min_val=0, max_val=1)
            with act.If(need > 0):
                def chunk(s, t, c, second):
                    if second:
                        act.wait_ge(below_ready, C * t + c + 1)
                        nc.scalar.activation(wm[:, FEAT:QS], below[:, :], ACT.Exp, scale=SCALE).then_inc(weight_ready, 1)

                walk(act, chunk)

        @block.tensor
        def _(pe):
            need = pe.value_load(flag[0:1, 0:1], min_val=0, max_val=1)
            with pe.If(need > 0):
                def chunk(s, t, c, second):
                    n = C * t + c
                    if not second:
                        pe.wait_ge(spread_ready, n + 1)
                        for h in range(HEADS):
                            tr = nc.tensor.transpose(spp[:, h, :], spread[:, h, :], ident[:, :])
                        tr.then_inc(spread_turned, 1)
                    else:
                        pe.wait_ge(hot_ready, n + 1)
                        nc.tensor.transpose(otp[:, 0:P], ehot[:, :], ident[:, :]).then_inc(hot_turned, 1)
                        pe.wait_ge(hot_t_ready, n + 1)
                        nc.tensor.matmul(mep[:, 0:HEADS], hot_t[:, :], gmax[:, :], start=True, stop=True).then_inc(edge_max, 1)
                        pe.wait_ge(wm_ready, n + 1)
                        nc.tensor.matmul(sump[:, 0:QS], ehot[:, :], wm[:, :], start=True, stop=True).then_inc(summed, 1)

                walk(pe, chunk)

        @block.vector
        def _(v):
            need = v.value_load(flag[0:1, 0:1], min_val=0, max_val=1)
            with v.If(need > 0):
                def before(t):
                    v.wait_ge(tile_own, TILE_STEPS * t + 1)
                    nc.vector.tensor_copy(base[:, :], tile_row[:, bass.ds(t, 1)]).then_inc(tile_own, 1)

                def chunk(s, t, c, second):
                    n = C * t + c
                    own, k = (b_own, B_STEPS * n) if second else (a_own, A_STEPS * n)
                    v.wait_ge(tile_own, TILE_STEPS * t + 2)
                    v.wait_ge(rows_here, 32 * (s + 1))
                    nc.vector.tensor_tensor(rel[:, :], ids[:, 1:2], base[:, :], ALU.subtract).then_inc(own, 1)
                    nc.vector.tensor_tensor(eqk[:, :], eq[:, 0:FEAT], ekv[:, 0:FEAT], ALU.mult).then_inc(own, 1)
                    v.wait_ge(own, k + 2)
                    nc.vector.tensor_reduce(score[:, :], eqk[:, :].rearrange("p (h d) -> p h d", d=HEAD), AX, ALU.add).then_inc(own, 1)
                    if not second:
                        nc.vector.tensor_scalar(ehot[:, :], colf[:, :], rel[:, 0:1], None, ALU.is_equal).then_inc(own, 1)
                        v.wait_ge(own, k + 4)
                        nc.vector.tensor_scalar(pos[:, :], score[:, :], 0.0, None, ALU.max).then_inc(own, 1)
                        v.wait_ge(own, k + 5)
                        nc.vector.tensor_tensor(spread[:, :, :], ehot[:, :].unsqueeze(1).broadcast_to([P, HEADS, P]),
                                                pos[:, :].unsqueeze(2).broadcast_to([P, HEADS, P]), ALU.mult).then_inc(spread_ready, 1)
                        v.wait_ge(spread_turned, n + 1)
                        nc.vector.tensor_reduce(peak[:, 0:4], spp[:, 0:4, :], AX, ALU.max).then_inc(own, 1)
                        nc.vector.tensor_reduce(peak[:, 4:8], spp[:, 4:8, :], AX, ALU.max).then_inc(own, 1)
                        v.wait_ge(own, k + 7)
                        nc.vector.tensor_tensor(gmax[:, :], gmax[:, :], peak[:, :], ALU.max).then_inc(own, 1)
                        v.wait_ge(own, k + 8)
                        nc.vector.tensor_copy(rel[:, :], base[:, :]).then_inc(ids_free, 1)
                    else:
                        nc.vector.tensor_scalar(ehot[:, :], colf[:, :], rel[:, 0:1], None, ALU.is_equal).then_inc(hot_ready, 1)
                        v.wait_ge(hot_turned, n + 1)
                        nc.vector.tensor_copy(hot_t[:, :], otp[:, 0:P]).then_inc(hot_t_ready, 1)
                        v.wait_ge(edge_max, n + 1)
                        v.wait_ge(own, k + 3)
                        nc.vector.tensor_tensor(score[:, :], score[:, :], mep[:, 0:HEADS], ALU.subtract).then_inc(own, 1)
                        v.wait_ge(own, k + 4)
                        nc.vector.tensor_scalar(below[:, :], score[:, :], 0.0, None, ALU.min).then_inc(below_ready, 1)
                        v.wait_ge(weight_ready, n + 1)
                        nc.vector.tensor_tensor(wm[:, 0:FEAT].rearrange("p (h d) -> p h d", d=HEAD),
                                                ekv[:, FEAT:2 * FEAT].rearrange("p (h d) -> p h d", d=HEAD),
                                                wm[:, FEAT:QS].unsqueeze(2).broadcast_to([P, HEADS, HEAD]), ALU.mult).then_inc(wm_ready, 1)
                        v.wait_ge(summed, n + 1)
                        nc.vector.tensor_tensor(acc[:, :], acc[:, :], sump[:, 0:QS], ALU.add).then_inc(own, 1)
                        v.wait_ge(own, k + 5)
                        nc.vector.tensor_copy(rel[:, :], base[:, :]).then_inc(ids_free, 1)

                def after(t, row):
                    k = TILE_STEPS * t + 2
                    nc.vector.tensor_scalar(inv[:, :], acc[:, FEAT:QS], 1e-8, None, ALU.add).then_inc(tile_own, 1)
                    v.wait_ge(tile_own, k + 1)
                    nc.vector.reciprocal(inv[:, :], inv[:, :]).then_inc(tile_own, 1)
                    v.wait_ge(tile_own, k + 2)
                    v.wait_ge(res_stored, 16 * (t + 1))
                    nc.vector.tensor_tensor(res[:, :].rearrange("p (h d) -> p h d", d=HEAD),
                                            acc[:, 0:FEAT].rearrange("p (h d) -> p h d", d=HEAD),
                                            inv[:, :].unsqueeze(2).broadcast_to([P, HEADS, HEAD]), ALU.mult).then_inc(res_ready, 1)
                    v.wait_ge(res_ready, t + 1)
                    nc.vector.memset(gmax[:, :], 0.0)
                    nc.vector.memset(acc[:, :], 0.0).then_inc(tile_own, 1)

                nc.vector.memset(gmax[:, :], 0.0)
                nc.vector.memset(acc[:, :], 0.0).then_inc(tile_own, 1)
                walk(v, chunk, before, after)


def finish(nc, env):
    (x, out, qs_d, kv_d, ident, colf, idx_src, idx_dst, slot_dst, sself, rstd_all, nbias_all, wo, w1, w2, vec, hb1,
     brow, pick) = (
        env[k] for k in ("x out qs_d kv_d ident colf idx_src idx_dst slot_dst sself rstd_all nbias_all "
                         "wo w1 w2 vec hb1 brow pick").split())
    N, SG = env["N"], env["SG"]
    G1, G2, B2 = 1, 3, 4
    SH = SGT * HEADS
    with ExitStack() as stack:
        sb, ps, sem = tensors(nc, stack)
        isrc = sb("isrc", [P, SGT], u32)
        idst = sb("idst", [P, SGT], u32)
        qg = sb("qg", [P, SGT, QS])
        kvg = sb("kvg", [P, SGT, 2 * FEAT])
        qk = sb("qk", [P, SGT, FEAT])
        tin = sb("tin", [P, 4, SGT, HEADS])
        own_t = sb("own_t", [SH, P])
        dst_t = sb("dst_t", [SH, P])
        same = sb("same", [SH, P + 1])
        last = sb("last", [SH, P])
        best = sb("best", [SH, P])
        run = sb("run", [SH, P])
        top = sb("top", [SH, P])
        less = sb("less", [SH, 2, P])
        ew = sb("ew", [SH, 2, P])
        den = sb("den", [SH, P])
        tback = sb("tback", [P, 3, P])
        pslot = sb("pslot", [P, SGT, HEADS])
        sel = sb("sel", [P, SGT, 2, HEADS])
        hot = sb("hot", [P, SGT, P])
        msg = sb("msg", [P, SGT, FEAT])
        alone = sb("alone", [P, 3, SGT, HEADS])
        pself = sb("pself", [P, SGT, HEADS])
        xg = [sb(f"x2g{b}", [P, GT, FEAT]) for b in range(2)]
        vrow = [sb(f"vrow{b}", [P, GT, FEAT]) for b in range(2)]
        xb = [sb(f"xb{b}", [P, GT, FEAT]) for b in range(2)]
        nrm = [sb(f"nrm{b}", [P, 2, GT]) for b in range(2)]
        hres = sb("hres", [P, GT, FEAT])
        agg = sb("agg", [P, GT, FEAT])
        at = sb("at", [P, KH, GT * P])
        mid = sb("mid", [P, GT, FEAT])
        ot = [sb(f"ot{k}", [P, KH, GT * P], fp32r) for k in range(2)]
        res2 = [sb(f"res2{b}", [P, GT, FEAT]) for b in range(2)]
        hid = sb("hid", [P, HM, GT * P])
        fin = [sb(f"fin{b}", [P, GT, FEAT]) for b in range(2)]
        stat = sb("stat_of", [P, 2 * GT, 6])
        tmp = sb("tmp_of", [P, 5, 2 * GT])
        tmpi = sb("tmpi_of", [P, 2 * GT], i32)
        rstd = sb("rstd_of", [P, 2 * GT])
        nbias = sb("nbias_of", [P, 2 * GT])
        tp = [ps(f"tq{k}", [P, 512]) for k in range(KH)]
        segp = [ps(f"segp{k}", [P, 2, FEAT]) for k in range(2)]
        yp = [ps(f"yp{k}", [P, 2, FEAT]) for k in range(2)]
        hp = ps("hp", [P, 512])
        ap = ps("ap", [P, 512])
        yb = [y.rearrange("p t c -> p (t c)") for y in (yp[0][:, :, :], yp[1][:, :, :])]
        chunk_bank = [hp[:, :], yb[0], yb[1], hp[:, :]]
        x_loaded = [sem("x2_loaded0"), sem("x2_loaded1")]
        v_loaded = [sem("v_loaded0"), sem("v_loaded1")]
        stored = [sem("out_stored0"), sem("out_stored1")]
        gathered = sem("slots_gathered")
        cleared = sem("gather_cleared")
        att_own = sem("attention_steps")
        n_own = sem("norm_steps")
        m_own = sem("scaling_steps")
        qk_ready = sem("products_ready")
        tin_ready = sem("scores_ready")
        tin_turned = sem("scores_turned")
        less_ready = sem("differences_ready")
        exp_ready = sem("exponentials_ready")
        tback_ready = sem("weights_ready")
        tback_turned = sem("weights_turned")
        hot_ready = sem("one_hot_ready")
        msg_ready = sem("messages_ready")
        sel_turned = sem("loops_selected")
        pself_ready = sem("loop_weights_ready")
        nrm_ready = sem("norm_staged")
        h_ready = sem("h_again")
        xb_ready = sem("x_plus_b2")
        vself_ready = sem("own_values_weighted")
        seg_done = sem("segments_summed")
        agg_ready = sem("agg_ready")
        agg_turned = sem("agg_turned")
        at_ready = sem("agg_turned_out")
        wo_done = sem("projected_out")
        mid_sum = sem("residual_summed")
        z1_ready = sem("normed1")
        mid_scaled = sem("mid_scaled")
        mid_turned = sem("mid_turned")
        ot_hi = sem("ot_high")
        ot_lo = sem("ot_low")
        chunk_done = sem("hidden_chunk")
        gelu_done = sem("gelu_done")
        ffn_done = sem("ffn_done")
        fin_sum = sem("residual2_summed")
        z2_ready = sem("normed2")
        fin_scaled = sem("out_scaled")
        fin_ready = [sem("out_ready0"), sem("out_ready1")]
        block = stack.enter_context(nc.Block())
        STEPS = LN_STEPS + 2
        ATT = 20

        def is_first(i, b=0):
            return isinstance(i, int) and i == 0 and b == 0

        def is_last(i):
            return isinstance(i, int) and i == SG - 1

        def before(i, b):
            return (i, 0, 2 * i) if b else (i - 1, 1, 2 * i - 1)

        def every(eng, body):
            body(0)
            with eng.Fori(1, SG - 1) as i:
                body(i)
            body(SG - 1)

        def rows(i, b):
            first = (N - SGN) if is_last(i) else i * SGN
            return bass.ds(first + b * GT * P, GT * P)

        @block.sync
        def _(sp):
            def load(i, b):
                g = 2 * i + b
                if not (isinstance(i, int) and i == 0):
                    sp.wait_ge(h_ready, g - 1)
                    sp.wait_ge(xb_ready, g - 1)
                sp.dma_start(xg[b][:, :, :], x[rows(i, b), :].rearrange("(j p) c -> p j c", p=P)).then_inc(x_loaded[b], 16)
                if not (isinstance(i, int) and i == 0):
                    sp.wait_ge(agg_ready, 2 * (g - 1))
                sp.dma_start(vrow[b][:, :, :], kv_d[rows(i, b), FEAT:2 * FEAT].rearrange("(j p) c -> p j c", p=P)).then_inc(v_loaded[b], 16)

            def store(i, b):
                sp.wait_ge(fin_ready[b], i + 1)
                sp.dma_start(out[rows(i, b), :].rearrange("(j p) c -> p j c", p=P), fin[b][:, :, :]).then_inc(stored[b], 16)

            for b in range(2):
                sp.sem_inc(stored[b], 16)
            load(0, 0)
            load(0, 1)
            load(1, 0)
            with sp.Fori(1, SG - 2) as i:
                load(i, 1)
                store(i - 1, 0)
                load(i + 1, 0)
                store(i - 1, 1)
            load(SG - 2, 1)
            store(SG - 3, 0)
            load(SG - 1, 0)
            store(SG - 3, 1)
            load(SG - 1, 1)
            store(SG - 2, 0)
            store(SG - 2, 1)
            for b in range(2):
                sp.wait_ge(stored[b], 16 * SG)
            store(SG - 1, 0)
            store(SG - 1, 1)
            for b in range(2):
                sp.wait_ge(stored[b], 16 * (SG + 1))

        @block.gpsimd
        def _(pool):
            top_row = pool.to_reg(N - 1)
            EARLY = 1

            def gather_q(i):
                for t in range(SGT):
                    nc.gpsimd.indirect_dma_start(
                        out=qg[:, t, :], out_offset=None, in_=qs_d,
                        in_offset=bass.IndirectOffsetOnAxis(ap=idst[:, t:t + 1], axis=0),
                        bounds_check=top_row, oob_is_err=False).then_inc(gathered, 16)

            def gather_kv(i, tiles):
                for t in tiles:
                    nc.gpsimd.indirect_dma_start(
                        out=kvg[:, t, :], out_offset=None, in_=kv_d,
                        in_offset=bass.IndirectOffsetOnAxis(ap=isrc[:, t:t + 1], axis=0),
                        bounds_check=top_row, oob_is_err=False).then_inc(gathered, 16)

            def finish_group(i):
                pool.wait_ge(fin_scaled, i + 1)
                pool.wait_ge(xb_ready, 2 * i + 1)
                nc.gpsimd.tensor_tensor(fin[0][:, :, :], fin[0][:, :, :], xb[0][:, :, :], ALU.add).then_inc(fin_ready[0], 1)

            def weigh_own(i, b):
                pool.wait_ge(v_loaded[b], 16 * (i + 1))
                pool.wait_ge(pself_ready, i + 1)
                vh = vrow[b][:, :, :].rearrange("p j (h d) -> p (j h) d", d=HEAD)
                ph = pself[:, GT * b:GT * b + GT, :].rearrange("p j h -> p (j h)").unsqueeze(2).broadcast_to([P, GT * HEADS, HEAD])
                nc.gpsimd.tensor_tensor(vh, vh, ph, ALU.mult).then_inc(vself_ready, 1)

            def last_residual(i, b):
                pool.wait_ge(x_loaded[b], 16 * (i + 1))
                if not (isinstance(i, int) and i == 0):
                    pool.wait_ge(fin_ready[b], i)
                nc.gpsimd.tensor_tensor(xb[b][:, :, :], xg[b][:, :, :], vec[:, B2, :].unsqueeze(1).broadcast_to([P, GT, FEAT]),
                                        ALU.add).then_inc(xb_ready, 1)

            def scale_mid(i, b):
                g = 2 * i + b
                pool.wait_ge(z1_ready, g + 1)
                if not (isinstance(i, int) and i == 0):
                    pool.wait_ge(fin_sum, 2 * (g - 1))
                nc.gpsimd.tensor_tensor(res2[b][:, :, :], mid[:, :, :], vec[:, G1, :].unsqueeze(1).broadcast_to([P, GT, FEAT]),
                                        ALU.mult).then_inc(mid_scaled, 1)

            def qk_products(i):
                if not is_first(i):
                    pool.wait_ge(tin_ready, i)
                pool.wait_ge(gathered, 16 * 2 * SGT * (i + 1))
                nc.gpsimd.tensor_tensor(qk[:, :, :], qg[:, :, 0:FEAT], kvg[:, :, 0:FEAT], ALU.mult).then_inc(qk_ready, 1)

            nc.gpsimd.memset(qg[:, :, :], 0.0)
            nc.gpsimd.memset(kvg[:, :, :], 0.0).then_inc(cleared, 1)
            pool.wait_ge(cleared, 2)
            gather_q(0)
            gather_kv(0, range(SGT))
            qk_products(0)
            pool.wait_ge(tin_ready, 1)
            last_residual(0, 0)
            gather_q(1)

            def body(i):
                if not is_first(i):
                    if not is_last(i):
                        pool.wait_ge(msg_ready, i + 1)
                    scale_mid(i - 1, 1)
                if not is_last(i):
                    if is_first(i):
                        pool.wait_ge(msg_ready, 1)
                    gather_kv(i + 1, range(0, EARLY))
                weigh_own(i, 0)
                if not is_last(i):
                    gather_kv(i + 1, range(EARLY, SGT))
                if not is_first(i):
                    last_residual(i - 1, 1)
                if not is_last(i):
                    qk_products(i + 1)
                weigh_own(i, 1)
                if not is_first(i):
                    finish_group(i - 1)
                    last_residual(i, 0)
                if not is_last(i):
                    pool.wait_ge(tin_ready, i + 2)
                scale_mid(i, 0)

            body(0)
            gather_q(2)
            body(1)
            gather_q(3)
            with pool.Fori(2, SG - 2) as i:
                body(i)
                gather_q(i + 2)
            body(SG - 2)
            body(SG - 1)
            last_residual(SG - 1, 1)
            scale_mid(SG - 1, 1)
            finish_group(SG - 1)

        @block.scalar
        def _(act):
            def h_again(i, b):
                g = 2 * i + b
                act.wait_ge(nrm_ready, g + 1)
                act.wait_ge(x_loaded[b], 16 * (i + 1))
                if not is_first(i, b):
                    act.wait_ge(mid_sum, 2 * g)
                for j in range(GT):
                    ins = nc.scalar.activation(hres[:, j, :], xg[b][:, j, :], ACT.Relu, bias=nrm[b][:, 1, j:j + 1],
                                               scale=nrm[b][:, 0, j:j + 1])
                ins.then_inc(h_ready, 1)

            def gelus(gp, chunks, first=False):
                for m in chunks:
                    act.wait_ge(chunk_done, HM * gp + m + 1)
                    if not first and m == 0:
                        act.wait_ge(ffn_done, 2 * gp)
                    nc.scalar.activation(hid[:, m, :], chunk_bank[m], ACT.Gelu, bias=hb1[:, m:m + 1]).then_inc(gelu_done, 1)

            def agg_out(i, b):
                g = 2 * i + b
                for k in range(KH):
                    act.wait_ge(agg_turned, KH * g + k + 1)
                    if not is_first(i, b) and k == 0:
                        act.wait_ge(wo_done, 2 * g)
                    nc.scalar.activation(at[:, k, :], tp[k][:, :], ACT.Copy).then_inc(at_ready, 1)

            def exps(i):
                act.wait_ge(less_ready, i + 1)
                nc.scalar.activation(ew[:, :, :], less[:, :, :], ACT.Exp, scale=SCALE)
                nc.scalar.activation(alone[:, 1, :, :], alone[:, 0, :, :], ACT.Exp, scale=SCALE).then_inc(exp_ready, 1)

            def norm1(i, b):
                act.wait_ge(n_own, STEPS * (2 * i + b + 1))
                for j in range(GT):
                    ins = nc.scalar.activation(mid[:, j, :], mid[:, j, :], ACT.Identity, bias=nbias[:, j:j + 1], scale=rstd[:, j:j + 1])
                ins.then_inc(z1_ready, 1)

            def mid_high(gp, first):
                for k in range(KH):
                    act.wait_ge(mid_turned, KH * gp + k + 1)
                    if not first and k == 0:
                        act.wait_ge(chunk_done, HM * gp)
                    nc.scalar.activation(ot[0][:, k, :], yb[k], ACT.Copy).then_inc(ot_hi, 1)

            def norm2(b):
                for j in range(GT):
                    ins = nc.scalar.activation(fin[b][:, j, :], fin[b][:, j, :], ACT.Identity, bias=nbias[:, GT + j:GT + j + 1],
                                               scale=rstd[:, GT + j:GT + j + 1])
                ins.then_inc(z2_ready, 1)

            exps(0)
            h_again(0, 0)

            def body(i):
                for b in range(2):
                    _, bp, gp = before(i, b)
                    if not is_first(i, b):
                        mid_high(gp, is_first(i))
                    agg_out(i, b)
                    if b == 1 and not is_last(i):
                        exps(i + 1)
                    if not is_first(i, b):
                        gelus(gp, range(HM), is_first(i))
                    norm1(i, b)
                    if not is_first(i):
                        norm2(b)
                    if b == 0:
                        h_again(i, 1)
                    elif not is_last(i):
                        h_again(i + 1, 0)

            every(act, body)
            g = 2 * SG - 1
            mid_high(g, False)
            gelus(g, range(HM))
            act.wait_ge(n_own, STEPS * (g + 2))
            norm2(0)
            act.wait_ge(n_own, STEPS * (g + 3))
            norm2(1)

        @block.vector
        def _(v):
            def stage_norm(i, b):
                g = 2 * i + b
                if not (isinstance(i, int) and i == 0):
                    v.wait_ge(h_ready, g - 1)
                nc.vector.tensor_copy(nrm[b][:, 0, :], rstd_all[:, bass.ds(SGT * i + GT * b, GT)])
                nc.vector.tensor_copy(nrm[b][:, 1, :], nbias_all[:, bass.ds(SGT * i + GT * b, GT)]).then_inc(nrm_ready, 1)

            def att_scores(i):
                v.wait_ge(gathered, 16 * 2 * SGT * (i + 1))
                if not is_first(i):
                    v.wait_ge(tin_turned, i)
                nc.vector.tensor_copy(isrc[:, :], idx_src[:, bass.ds(SGT * i + SGT, SGT)])
                nc.vector.tensor_copy(idst[:, :], idx_dst[:, bass.ds(SGT * i + SGT, SGT)])
                nc.vector.tensor_copy(tin[:, 1, :, :], qg[:, :, FEAT:QS])
                nc.vector.tensor_copy(tin[:, 2, :, :], slot_dst[:, bass.ds(SGT * i, SGT)].unsqueeze(2).broadcast_to([P, SGT, HEADS]))
                v.wait_ge(qk_ready, i + 1)
                nc.vector.tensor_reduce(tin[:, 0, :, :], qk[:, :, :].rearrange("p t (h d) -> p t h d", d=HEAD), AX,
                                        ALU.add).then_inc(tin_ready, 1)

            def att_max(i):
                c = ATT * i
                v.wait_ge(tin_turned, i + 1)
                nc.vector.tensor_copy(own_t[:, :], ap[0:SH, P:2 * P]).then_inc(att_own, 1)
                nc.vector.tensor_copy(dst_t[:, :], ap[0:SH, 2 * P:3 * P]).then_inc(att_own, 1)
                v.wait_ge(att_own, c + 2)
                nc.vector.tensor_tensor(same[:, 1:P], dst_t[:, 1:P], dst_t[:, 0:P - 1], ALU.is_equal).then_inc(att_own, 1)
                nc.vector.scalar_tensor_tensor(best[:, :], ap[0:SH, 0:P], 0.0, own_t[:, :], ALU.max, ALU.max).then_inc(att_own, 1)
                nc.vector.tensor_scalar(alone[:, 0, :, :], sself[:, bass.ds(SGT * i, SGT), :], 0.0, None, ALU.min).then_inc(att_own, 1)
                v.wait_ge(att_own, c + 5)
                nc.vector.tensor_tensor_scan(run[:, :], same[:, 0:P], best[:, :], 0.0, ALU.mult, ALU.max).then_inc(att_own, 1)
                nc.vector.tensor_scalar(last[:, :], same[:, 1:P + 1], -1.0, 1.0, ALU.mult, ALU.add).then_inc(att_own, 1)
                v.wait_ge(att_own, c + 7)
                nc.vector.tensor_tensor_scan(top[:, ::-1], same[:, P:0:-1], run[:, ::-1], 0.0, ALU.mult, ALU.max).then_inc(att_own, 1)
                v.wait_ge(att_own, c + 8)
                nc.vector.tensor_tensor(less[:, 0, :], ap[0:SH, 0:P], top[:, :], ALU.subtract)
                nc.vector.tensor_tensor(less[:, 1, :], own_t[:, :], top[:, :], ALU.subtract).then_inc(less_ready, 1)

            def att_weights(i):
                c = ATT * i + 8
                v.wait_ge(exp_ready, i + 1)
                nc.vector.tensor_tensor_scan(run[:, :], same[:, 0:P], ew[:, 0, :], 0.0, ALU.mult, ALU.add).then_inc(att_own, 1)
                nc.vector.tensor_scalar(alone[:, 2, :, :], alone[:, 1, :, :], 1e-8, None, ALU.add).then_inc(att_own, 1)
                v.wait_ge(att_own, c + 2)
                nc.vector.tensor_tensor_scan(top[:, ::-1], same[:, P:0:-1], run[:, ::-1], 0.0, ALU.mult, ALU.max).then_inc(att_own, 1)
                nc.vector.reciprocal(alone[:, 2, :, :], alone[:, 2, :, :]).then_inc(att_own, 1)
                v.wait_ge(att_own, c + 4)
                nc.vector.scalar_tensor_tensor(den[:, :], top[:, :], 1e-8, ew[:, 1, :], ALU.add, ALU.add).then_inc(att_own, 1)
                nc.vector.tensor_tensor(alone[:, 0, :, :], alone[:, 1, :, :], alone[:, 2, :, :], ALU.mult).then_inc(att_own, 1)
                v.wait_ge(att_own, c + 6)
                nc.vector.reciprocal(den[:, :], den[:, :]).then_inc(att_own, 1)
                v.wait_ge(att_own, c + 7)
                if not is_first(i):
                    v.wait_ge(tback_turned, i)
                nc.vector.tensor_tensor(tback[0:SH, 0, :], ew[:, 0, :], den[:, :], ALU.mult).then_inc(att_own, 1)
                nc.vector.tensor_tensor(tback[0:SH, 1, :], ew[:, 1, :], den[:, :], ALU.mult).then_inc(att_own, 1)
                v.wait_ge(att_own, c + 9)
                nc.vector.tensor_tensor(tback[0:SH, 1, :], tback[0:SH, 1, :], last[:, :], ALU.mult)
                nc.vector.tensor_copy(tback[0:SH, 2, :], last[:, :]).then_inc(tback_ready, 1)

            def one_hot(i, t):
                if t == 0 and not is_first(i):
                    v.wait_ge(sel_turned, i)
                    v.wait_ge(seg_done, 4 * i)
                nc.vector.tensor_scalar(hot[:, t, :], colf[:, :], tin[:, 2, t, 0:1], None, ALU.is_equal)

            def att_messages(i):
                c = ATT * i + 17
                v.wait_ge(tback_turned, i + 1)
                nc.vector.tensor_copy(pslot[:, :, :], ap[:, 0:SH].rearrange("p (t h) -> p t h", h=HEADS)).then_inc(att_own, 1)
                if not is_first(i):
                    v.wait_ge(sel_turned, i)
                    v.wait_ge(seg_done, 4 * i)
                nc.vector.tensor_copy(sel[:, :, 0, :], ap[:, SH:2 * SH].rearrange("p (t h) -> p t h", h=HEADS))
                nc.vector.tensor_copy(sel[:, :, 1, :], ap[:, 2 * SH:3 * SH].rearrange("p (t h) -> p t h", h=HEADS)).then_inc(hot_ready, 1)
                v.wait_ge(att_own, c + 1)
                nc.vector.tensor_tensor(
                    msg[:, :, :].rearrange("p t (h d) -> p t h d", d=HEAD),
                    kvg[:, :, FEAT:2 * FEAT].rearrange("p t (h d) -> p t h d", d=HEAD),
                    pslot[:, :, :].unsqueeze(3).broadcast_to([P, SGT, HEADS, HEAD]), ALU.mult).then_inc(msg_ready, 1)

            def att_own_weights(i):
                c = ATT * i + 18
                got = ap[:, 256:256 + 2 * SH].rearrange("p (t s h) -> p t s h", s=2, h=HEADS)
                v.wait_ge(sel_turned, i + 1)
                nc.vector.tensor_scalar(alone[:, 1, :, :], got[:, :, 1, :], -1.0, 1.0, ALU.mult, ALU.add).then_inc(att_own, 1)
                v.wait_ge(att_own, c + 1)
                nc.vector.tensor_tensor(alone[:, 2, :, :], alone[:, 1, :, :], alone[:, 0, :, :], ALU.mult).then_inc(att_own, 1)
                v.wait_ge(att_own, c + 2)
                if not is_first(i):
                    v.wait_ge(vself_ready, 2 * i)
                nc.vector.tensor_tensor(pself[:, :, :], alone[:, 2, :, :], got[:, :, 0, :], ALU.add).then_inc(pself_ready, 1)

            def sum_agg(i, b):
                g = 2 * i + b
                v.wait_ge(vself_ready, g + 1)
                if not is_first(i, b):
                    v.wait_ge(agg_turned, KH * g)
                for k in range(2):
                    v.wait_ge(seg_done, 2 * g + k + 1)
                    nc.vector.tensor_tensor(agg[:, 2 * k:2 * k + 2, :], segp[k][:, :, :], vrow[b][:, 2 * k:2 * k + 2, :], ALU.add).then_inc(agg_ready, 1)

            def sum_mid(i, b):
                g = 2 * i + b
                v.wait_ge(h_ready, g + 1)
                if not is_first(i, b):
                    v.wait_ge(mid_turned, KH * g)
                    v.wait_ge(mid_scaled, g)
                for k in range(2):
                    v.wait_ge(wo_done, 2 * g + k + 1)
                    nc.vector.tensor_tensor(mid[:, 2 * k:2 * k + 2, :], segp[k][:, :, :], hres[:, 2 * k:2 * k + 2, :], ALU.add).then_inc(mid_sum, 1)
                v.wait_ge(mid_sum, 2 * g + 2)
                for j in range(GT):
                    ins = nc.vector.bn_stats(stat[:, j, :], mid[:, j, :])
                ins.then_inc(n_own, 2 if is_first(i) else 1)

            def roots(g, lo, hi, meanwhile=None):
                v.wait_ge(n_own, STEPS * g + 2)
                inverse_deviation(nc, v, n_own, STEPS * g + 2, stat[:, lo:hi, :], tmp[:, :, lo:hi], tmpi[:, lo:hi], rstd[:, lo:hi], nbias[:, lo:hi],
                                  meanwhile)

            def mid_low(i, b):
                g = 2 * i + b
                for k in range(KH):
                    v.wait_ge(ot_hi, KH * g + k + 1)
                    nc.vector.tensor_tensor(ot[1][:, k, :], yb[k], ot[0][:, k, :].bitcast(fp32), ALU.subtract).then_inc(ot_lo, 1)

            def sum_fin(i, b):
                gp = 2 * i + b - 2
                v.wait_ge(mid_scaled, gp + 1)
                v.wait_ge(stored[b], 16 * i)
                for k in range(2):
                    v.wait_ge(ffn_done, 2 * gp + k + 1)
                    nc.vector.tensor_tensor(fin[b][:, 2 * k:2 * k + 2, :], yp[k][:, :, :], res2[b][:, 2 * k:2 * k + 2, :], ALU.add).then_inc(fin_sum, 1)

            def stats_fin(i, b):
                v.wait_ge(fin_sum, 2 * (2 * i + b - 1))
                for j in range(GT):
                    ins = nc.vector.bn_stats(stat[:, GT + j, :], fin[b][:, j, :])
                ins.then_inc(n_own, 2 if isinstance(i, int) and i == SG else 1)

            def finish_group(i, b):
                gp = 2 * i + b - 2
                v.wait_ge(z2_ready, gp + 1)
                scaled = nc.vector.tensor_tensor(fin[b][:, :, :], fin[b][:, :, :], vec[:, G2, :].unsqueeze(1).broadcast_to([P, GT, FEAT]), ALU.mult)
                if b == 0:
                    scaled.then_inc(fin_scaled, 1)
                else:
                    scaled.then_inc(m_own, 1)
                    v.wait_ge(m_own, i)
                    v.wait_ge(xb_ready, gp + 1)
                    nc.vector.tensor_tensor(fin[b][:, :, :], fin[b][:, :, :], xb[b][:, :, :], ALU.add).then_inc(fin_ready[b], 1)

            nc.vector.memset(same[:, 0:1], 0.0)
            nc.vector.memset(tin[:, 3, :, :], 0.0)
            nc.vector.memset(tback[:, :, :], 0.0)
            nc.vector.tensor_copy(isrc[:, :], idx_src[:, 0:SGT])
            nc.vector.tensor_copy(idst[:, :], idx_dst[:, 0:SGT])
            nc.vector.memset(same[:, P:P + 1], 0.0).then_inc(cleared, 1)
            v.wait_ge(cleared, 2)
            stage_norm(0, 0)
            att_scores(0)
            att_max(0)
            att_weights(0)
            for t in range(SGT):
                one_hot(0, t)
            att_messages(0)
            att_own_weights(0)

            def body(i):
                for b in range(2):
                    ip, bp, gp = before(i, b)
                    g = 2 * i + b
                    attend = b == 1 and not is_last(i)
                    if not is_first(i):
                        sum_fin(i, b)
                        stats_fin(i, b)
                    if not is_first(i, b):
                        mid_low(ip, bp)
                    sum_agg(i, b)
                    if attend:
                        att_max(i + 1)
                    if b == 0:
                        stage_norm(i, 1)
                    elif not is_last(i):
                        stage_norm(i + 1, 0)
                    if b == 0 and not is_first(i) and not (isinstance(i, int) and i == 1):
                        finish_group(i - 1, 1)
                    if attend:
                        att_weights(i + 1)
                    sum_mid(i, b)
                    roots(g, 0, GT if is_first(i) else 2 * GT, (lambda step: one_hot(i + 1, step)) if attend else None)
                    if attend:
                        for t in range(LN_CHAIN, SGT):
                            one_hot(i + 1, t)
                        att_messages(i + 1)
                    if b == 0 and not is_last(i):
                        att_scores(i + 1)
                    if b == 0 and not is_first(i):
                        finish_group(i, 0)
                    if attend:
                        att_own_weights(i + 1)

            body(0)
            body(1)
            with v.Fori(2, SG - 1) as i:
                body(i)
            body(SG - 1)
            sum_fin(SG, 0)
            mid_low(SG - 1, 1)
            stats_fin(SG, 0)
            finish_group(SG - 1, 1)
            roots(2 * SG, GT, 2 * GT)
            finish_group(SG, 0)
            sum_fin(SG, 1)
            stats_fin(SG, 1)
            roots(2 * SG + 1, GT, 2 * GT)
            finish_group(SG, 1)

        @block.tensor
        def _(pe):
            def product(out_ap, pairs):
                n = 0
                for lhs, rhs in pairs:
                    for a, c in ((0, 0), (0, 1), (1, 0)):
                        mm = nc.tensor.matmul(out_ap, lhs[a], rhs[c], start=n == 0, stop=n == 3 * len(pairs) - 1)
                        n += 1
                return mm

            def turn_scores(i):
                pe.wait_ge(tin_ready, i + 1)
                if not is_first(i):
                    pe.wait_ge(pself_ready, i)
                for k in range(3):
                    tr = nc.tensor.transpose(ap[:, k * P:(k + 1) * P], tin[:, k:k + 2, :, :].rearrange("p k t h -> p (k t h)"), ident[:, :])
                tr.then_inc(tin_turned, 1)

            def turn_weights(i):
                pe.wait_ge(tback_ready, i + 1)
                for k in range(3):
                    tr = nc.tensor.transpose(ap[:, k * SH:k * SH + P], tback[:, k, :], ident[:, :])
                tr.then_inc(tback_turned, 1)

            def select_loops(i):
                pe.wait_ge(hot_ready, i + 1)
                for t in range(SGT):
                    mm = nc.tensor.matmul(ap[:, 256 + 16 * t:272 + 16 * t], hot[:, t, :],
                                          sel[:, t, :, :].rearrange("p s h -> p (s h)"), start=True, stop=True)
                mm.then_inc(sel_turned, 1)

            def segments(i, b):
                g = 2 * i + b
                pe.wait_ge(msg_ready, i + 1)
                for j in range(GT):
                    if j % 2 == 0 and not is_first(i, b):
                        pe.wait_ge(mid_sum, 2 * (g - 1) + j // 2 + 1)
                    mm = nc.tensor.matmul(segp[j // 2][:, j % 2, :], hot[:, GT * b + j, :], msg[:, GT * b + j, :], start=True, stop=True)
                    if j % 2:
                        mm.then_inc(seg_done, 1)

            def turn_agg(i, b):
                g = 2 * i + b
                pe.wait_ge(agg_ready, 2 * g + 2)
                if not is_first(i, b):
                    pe.wait_ge(at_ready, KH * g)
                for k in range(KH):
                    for j in range(GT):
                        tr = nc.tensor.transpose(tp[k][:, j * P:(j + 1) * P], agg[:, j, k * P:(k + 1) * P], ident[:, :])
                    tr.then_inc(agg_turned, 1)

            def project_out(i, b):
                g = 2 * i + b
                pe.wait_ge(at_ready, KH * (g + 1))
                for j in range(GT):
                    nc.tensor.matmul(segp[j // 2][:, j % 2, :], pick[:, :], brow[:, 0, :], start=True, stop=False)
                    for k in range(KH):
                        mm = nc.tensor.matmul(segp[j // 2][:, j % 2, :], at[:, k, j * P:(j + 1) * P], wo[:, k, :], start=False, stop=k == KH - 1)
                    if j % 2:
                        mm.then_inc(wo_done, 1)

            def turn_mid(gp, first):
                pe.wait_ge(z1_ready, gp + 1)
                for k in range(KH):
                    if not first:
                        pe.wait_ge(fin_sum, 2 * (gp - 1) + k + 1)
                    for j in range(GT):
                        tr = nc.tensor.transpose(yp[k][:, j // 2, P * (j % 2):P * (j % 2) + P], mid[:, j, k * P:(k + 1) * P], ident[:, :])
                    tr.then_inc(mid_turned, 1)

            def hidden(gp, chunks, first=False):
                for m in chunks:
                    if m == 0:
                        pe.wait_ge(ot_lo, KH * (gp + 1))
                        if not first:
                            pe.wait_ge(gelu_done, HM * gp)
                    elif m == 3:
                        pe.wait_ge(gelu_done, HM * gp + 1)
                    product(chunk_bank[m],
                            [([w1[a][:, k, m * P:(m + 1) * P] for a in range(2)], [ot[a][:, k, :] for a in range(2)])
                             for k in range(KH)]).then_inc(chunk_done, 1)

            def feed(gp, tiles):
                for j in tiles:
                    if j == 0:
                        pe.wait_ge(gelu_done, HM * gp + 3)
                    nc.tensor.matmul(yp[j // 2][:, j % 2, :], pick[:, :], brow[:, 1, :], start=True, stop=False)
                    for m in range(HM):
                        if j == 0 and m == 3:
                            pe.wait_ge(gelu_done, HM * (gp + 1))
                        mm = nc.tensor.matmul(yp[j // 2][:, j % 2, :], hid[:, m, j * P:(j + 1) * P], w2[:, m, :],
                                              start=False, stop=m == HM - 1)
                    if j % 2:
                        mm.then_inc(ffn_done, 1)

            turn_scores(0)
            turn_weights(0)
            select_loops(0)

            def body(i):
                for b in range(2):
                    ip, bp, gp = before(i, b)
                    attend = b == 1 and not is_last(i)
                    if not is_first(i, b):
                        turn_mid(gp, is_first(i))
                    if attend:
                        turn_scores(i + 1)
                    segments(i, b)
                    if not is_first(i, b):
                        hidden(gp, (0,), is_first(i))
                    turn_agg(i, b)
                    if not is_first(i, b):
                        hidden(gp, (1,))
                    project_out(i, b)
                    if not is_first(i, b):
                        hidden(gp, (2, 3))
                    if attend:
                        turn_weights(i + 1)
                    if not is_first(i, b):
                        feed(gp, range(GT - 1))
                    if attend:
                        select_loops(i + 1)
                    if not is_first(i, b):
                        feed(gp, (GT - 1,))

            every(pe, body)
            g = 2 * SG - 1
            turn_mid(g, False)
            hidden(g, range(HM))
            feed(g, range(GT))


_INS = ["x", "src", "dst", "L0_gnn_Wq", "L0_gnn_Wk", "L0_gnn_Wv", "L0_gnn_Wo_w", "L0_gnn_Wo_b", "L0_gnn_ln1_g",
        "L0_gnn_ln1_b", "L0_gnn_ln2_g", "L0_gnn_ln2_b", "L0_gnn_ffn_w1", "L0_gnn_ffn_b1", "L0_gnn_ffn_w2", "L0_gnn_ffn_b2"]


def kernel(**inputs):
    import numpy as np
    import concourse.bacc as bacc
    from concourse import mybir
    from concourse.bass_utils import run_bass_kernel_spmd

    nc = bacc.Bacc("TRN2", target_bir_lowering=False, num_devices=1)
    arrays, args = {}, []
    for name in _INS:
        a = np.ascontiguousarray(inputs[name])
        arrays["in_" + name] = a
        args.append(nc.dram_tensor("in_" + name, a.shape, mybir.dt.from_np(a.dtype), kind="ExternalInput").ap())
    shape = arrays["in_x"].shape
    args.append(nc.dram_tensor("out_0", shape, mybir.dt.float32, kind="ExternalOutput").ap())
    program(nc, *args)
    return run_bass_kernel_spmd(nc, [arrays], core_ids=[0]).results[0]["out_0"]
```
